# Optimizing a Trainium2 kernel written in Bass

```python
import numpy as np
import jax
import jax.numpy as jnp

def _softmax(x, axis=-1):
    return jax.nn.softmax(x, axis=axis)

def _gelu(x):
    return jax.nn.gelu(x, approximate=True)

def _silu(x):
    return jax.nn.silu(x)

def _sigmoid(x):
    return jax.nn.sigmoid(x)

def _layernorm(x, axis=-1, eps=1e-05):
    m = jnp.mean(x, axis=axis, keepdims=True)
    v = jnp.var(x, axis=axis, keepdims=True)
    return (x - m) / jnp.sqrt(v + eps)

def _scatter_add(tgt, idx, src, axis=0):
    return tgt.at[idx].add(src)

def _segment_sum(src, seg, n):
    return jax.ops.segment_sum(src, seg, n)
kernel_name = 'mk_adj_resnorm_d2_adj_r2_647af6'

def setup_inputs(seed: int=0):
    np.random.seed(seed)
    _w = jnp.asarray

    def _rec_inputs():
        import jax
        import jax.numpy as jnp
        _gk = jax.random.key(seed)
        x = -0.000929 + 1 * jax.random.normal(jax.random.fold_in(_gk, 1), (4096, 128), jnp.float32)
        _a = jax.random.bernoulli(jax.random.fold_in(_gk, 2), 0.00390625, (4096, 4096))
        adj = _a.astype(jnp.int32)
        return (x, adj)
    x, adj = _rec_inputs()

    def _L0_gnn_setup():
        import jax, jax.numpy as jnp
        import numpy as np
        from jax import lax
        N = 4096
        D = 128
        CHUNK = 128
        key = jax.random.key(seed)
        k1, k2 = jax.random.split(key)
        x = jax.random.normal(k1, (N, D), dtype=jnp.float32)
        adj = jax.random.randint(k2, (N, N), 0, 2, dtype=jnp.int32)
        return {'x': x, 'adj': adj}
    _L0_gnn_all = _L0_gnn_setup()
    _L0_gnn_in = {k: v for k, v in _L0_gnn_all.items() if k in ()}
    del _L0_gnn_all

    def _L1_gnn_setup():
        import jax, jax.numpy as jnp
        import numpy as np
        N = 4096
        IN = 128
        OUT = 128
        THR = 0.0001
        ALPHA = 0.2
        NEG = -1000000000.0
        key = jax.random.key(seed)
        k1, k2, k3, k4 = jax.random.split(key, 4)
        inp = jax.random.normal(k1, (N, IN), jnp.float32)
        W = jax.random.normal(k2, (IN, OUT), jnp.float32) * (1.414 * np.sqrt(2.0 / (IN + OUT)))
        a = jax.random.normal(k3, (2 * OUT, 1), jnp.float32) * (1.414 * np.sqrt(2.0 / (2 * OUT + 1)))
        adj = jax.random.randint(k4, (N, N), 0, 2, jnp.int32)
        return {'input': inp, 'W': W, 'a': a, 'adj': adj, 'M': N}
    _L1_gnn_all = _L1_gnn_setup()
    _L1_gnn_in = {k: v for k, v in _L1_gnn_all.items() if k in ('W', 'a')}
    del _L1_gnn_all
    return {'x': x, 'adj': adj, 'L1_gnn_W': _L1_gnn_in['W'], 'L1_gnn_a': _L1_gnn_in['a']}

def reference(x, adj, L1_gnn_W, L1_gnn_a):
    import jax
    import jax.numpy as jnp

    def _L0_gnn_ref(x, adj):
        import jax, jax.numpy as jnp
        import numpy as np
        from jax import lax
        N = 4096
        D = 128
        CHUNK = 128
        n, d = x.shape
        neg = jnp.finfo(x.dtype).min
        adj_chunks = adj.reshape(n // CHUNK, CHUNK, n)

        def step(carry, a):
            mask = a != 0
            masked = jnp.where(mask[:, :, None], x[None, :, :], neg)
            m = jnp.max(masked, axis=1)
            has_nbr = jnp.any(mask, axis=1)
            out = jnp.where(has_nbr[:, None], m, jnp.zeros((), x.dtype))
            return (carry, out)
        _, out = lax.scan(step, None, adj_chunks)
        return out.reshape(n, d)

    def _L1_gnn_ref(input, W, a, adj, M):
        import jax, jax.numpy as jnp
        import numpy as np
        N = 4096
        IN = 128
        OUT = 128
        THR = 0.0001
        ALPHA = 0.2
        NEG = -1000000000.0
        h = input @ W
        a_src = a[:OUT, 0]
        a_dst = a[OUT:, 0]
        e = jax.nn.leaky_relu((h[:M] @ a_src)[:, None] + (h @ a_dst)[None, :], negative_slope=ALPHA)
        valid = (adj[:M] > 0) & (h.sum(axis=1) != 0)[None, :]
        att = jax.nn.softmax(jnp.where(valid, e, NEG), axis=1)
        att = jnp.where(valid, att, 0.0)
        L = valid.sum(axis=1).astype(h.dtype)
        top = att.max(axis=1)
        attention = jnp.where(att >= THR, att, 0.0) * L[:, None]
        attention = jnp.where((top > THR)[:, None], attention, 0.0)
        h_prime = attention @ h
        return jax.nn.elu(h[:M] + h_prime)
    x = _layernorm(x + _L0_gnn_ref(x, adj), axis=-1)
    x = _layernorm(x + _L1_gnn_ref(x, L1_gnn_W, L1_gnn_a, adj, 4096), axis=-1)
    return x

_drawn_inputs = setup_inputs


def setup_inputs(seed=0):
    import zlib

    import numpy as np

    out = dict(_drawn_inputs(seed))
    spreads = {}
    factors = {}
    for name, (base, spread) in spreads.items():
        noise = np.random.default_rng([zlib.crc32(name.encode()), seed]).standard_normal(out[name].shape)
        drawn = base * np.exp(spread * noise) if base else spread * noise
        out[name] = jnp.asarray(drawn.astype(out[name].dtype))
    for name, factor in factors.items():
        out[name] = (out[name] * factor).astype(out[name].dtype)
    return out
```

```python
from contextlib import ExitStack

import concourse.bass as bass
import concourse.mybir as mybir

ALU = mybir.AluOpType
ACT = mybir.ActivationFunctionType
AX = mybir.AxisListType
F32, BF16, I32, U32 = mybir.dt.float32, mybir.dt.bfloat16, mybir.dt.int32, mybir.dt.uint32

P = 128
N = 4096
D = 128
TILES = N // P
GT = 8
GROUPS = TILES // GT
GROWS = GT * P
SEGMENT = 256
SEGMENTS = N // SEGMENT
CAND = 8 * SEGMENTS
LIST = 40
DEG, ROW, XCOL = LIST, LIST + 1, LIST + 2
REC = XCOL + D
SLOTS = [36, 22, 20, 18, 17, 16, 14, 13]
HCOLS = D + 2
GBUF = max(SLOTS) * HCOLS
EPS, THR, ALPHA, NEG = 1e-5, 1e-4, 0.2, -1e9
FMIN = -3.4028234663852886e38

UPTO = [sum(SLOTS[i] for i in range(o % 2, o + 1, 2)) for o in range(GT)]
PER_GROUP = [UPTO[GT - 2], UPTO[GT - 1]]

EXTRACT_STEPS = 15
SORT_STEPS = 12
CHECK_STEPS = 2
REDUCE_STEPS = 6
CHUNK = 32
CHUNKS = N // CHUNK
CHUNK_STEPS = 2
DENSE_MAX_STEPS = 6
DENSE_ATTEND_STEPS = 20
ATTEND_STEPS = 16
NORM_STEPS = 2


class Steps:

    def __init__(self, eng, sem, per, turn):
        self.eng, self.sem, self.per, self.base, self.k = eng, sem, per, turn * per, 0

    def __call__(self, instruction, passed=None):
        self.k += 1
        instruction.then_inc(self.sem, 1)
        self.eng.wait_ge(self.sem, self.base + self.k)
        if passed is not None:
            self.eng.sem_inc(passed, 1)

    def end(self):
        assert self.k == self.per, (self.k, self.per)


def build(nc, x, adj, W, a, out, lists, htab, x1_all, h_all, d_all, v_all):
    with ExitStack() as ctx:
        def sb(name, shape, dt=F32):
            return ctx.enter_context(nc.sbuf_tensor(name, shape, dt))

        def ps(name, shape):
            return ctx.enter_context(nc.psum_tensor(name, shape, F32))

        def sem(name):
            return ctx.enter_context(nc.semaphore(name))

        ident = sb("ident", [P, P])
        ones = sb("ones", [P, P])
        local_iota = sb("local_iota", [P, SEGMENT], BF16)
        seg_base = sb("seg_base", [P, CAND])
        row_id = sb("row_id", [P, TILES])
        tie = sb("tie", [P, GT])
        rank_base = sb("rank_base", [P, TILES])
        slot_iota = sb("slot_iota", [P, LIST])
        slots_of = sb("slots_of", [P, GT])
        w_aug = sb("w_aug", [P, D + 3])
        wT = sb("wT", [P, D])
        a3 = sb("a3", [P, 3])
        adj_in = sb("adj_in", [P, 2, N], I32)
        adj16 = sb("adj16", [P, 2, N], BF16)
        squares = sb("squares", [P, N], BF16)
        keys = sb("keys", [P, N], BF16)
        sums = sb("sums", [P, 2, GT])
        cand = sb("cand", [P, CAND])
        gkey = sb("gkey", [P, 2, CAND])
        top = sb("top", [P, LIST])
        pad = sb("pad", [P, LIST])
        flags = sb("flags", [P, 2, GT])
        flag_sum = sb("flag_sum", [P, GT])
        rec = sb("rec", [P, GT, REC])
        degkey = sb("degkey", [P, GT])
        diag = sb("diag", [P, GT, P])
        beaten = sb("beaten", [P, GROWS], BF16)
        rank = sb("rank", [P, GT])
        rank_u = sb("rank_u", [P, GT], U32)
        srt = sb("srt", [P, TILES, REC])
        idx = sb("idx", [P, GT, LIST], U32)
        rid = sb("rid", [P, GT], U32)
        G = sb("G", [P, 2, GBUF])
        nmax = sb("nmax", [P, D])
        has = sb("has", [P, 1])
        y0 = sb("y0", [P, D])
        stats = sb("stats", [P, 6])
        mv = sb("mv", [P, 2])
        std = sb("std", [P, 1])
        rstd = sb("rstd", [P, 1])
        x1w = sb("x1w", [P, GT, D])
        x1T = sb("x1T", [P, P])
        x1s = sb("x1s", [P, TILES, D])
        hown = sb("hown", [P, TILES, D + 1])
        hrow = sb("hrow", [P, GT, HCOLS])
        sgn = sb("sgn", [P, 1])
        vm = sb("vm", [P, LIST])
        cnt = sb("cnt", [P, 1])
        z = sb("z", [P, LIST])
        e = sb("e", [P, LIST])
        pen = sb("pen", [P, LIST])
        em = sb("em", [P, LIST])
        mx = sb("mx", [P, 1])
        nmx = sb("nmx", [P, 1])
        pe_ = sb("pexp", [P, LIST])
        zs = sb("zs", [P, 1])
        rz = sb("rz", [P, 1])
        att = sb("att", [P, LIST])
        topa = sb("topa", [P, 1])
        gate = sb("gate", [P, 1])
        wgt = sb("wgt", [P, LIST])
        hsum = sb("hsum", [P, D])
        u = sb("u", [P, D])
        upos = sb("upos", [P, D])
        uneg = sb("uneg", [P, D])
        uexp = sb("uexp", [P, D])
        yw = sb("yw", [P, GT, D])
        mvs = sb("mvs", [P, GT, 2])
        stds = sb("stds", [P, GT])
        rstds = sb("rstds", [P, GT])

        flag = sb("flag", [P, 1])
        flag_int = sb("flag_int", [P, 1], I32)
        s_all = sb("s_all", [P, TILES])
        d_has = sb("d_has", [P, 1])
        d_acc = sb("d_acc", [P, D])
        d_max = sb("d_max", [P, D])
        d_x = sb("d_x", [P, D])
        d_h = sb("d_h", [P, D + 3])
        h_own = sb("h_own", [P, D])
        d_wT = sb("d_wT", [P, 2, P])
        d_adj = adj_in[:, 0, :]
        d_bias = srt[:, :, :].rearrange("p t r -> p (t r)")[:, 0:N]
        d_sum = x1s[:, :, :].rearrange("p t d -> p (t d)")
        d_z, d_vm = d_bias, d_sum
        d_p = adj_in[:, 1, :].bitcast(F32)
        d_rows, v_rows = G[:, 0, 0:N], G[:, 1, 0:N]
        h_rows = hown[:, :, :].rearrange("p t d -> p (t d)")[:, 0:N].rearrange("p (t d) -> p t d", d=D)

        psR = ps("psR", [P, GROWS])
        psT = ps("psT", [P, 512])
        psH = ps("psH", [P, 512])
        psW = ps("psW", [P, 512])

        consts_pool = sem("consts_pool")
        consts_dve = sem("consts_dve")
        weights_loaded = sem("weights_loaded")
        wT_ready = sem("wT_ready")
        wT_copied = sem("wT_copied")
        wa_ready = sem("wa_ready")
        w_aug_ready = sem("w_aug_ready")
        adj_loaded = [sem(f"adj_loaded{b}") for b in range(2)]
        x_loaded = sem("x_loaded")
        adj_free = sem("adj_free")
        converted = sem("converted")
        keyed = sem("keyed")
        extract_step = sem("extract_step")
        sort_step = sem("sort_step")
        check_step = sem("check_step")
        diag_ready = sem("diag_ready")
        degs_spread = sem("degs_spread")
        ranked = sem("ranked")
        lists_stored = sem("lists_stored")
        sorted_loaded = sem("sorted_loaded")
        idx_ready = sem("idx_ready")
        gathered = [sem(f"gathered{b}") for b in range(2)]
        buffer_free = sem("buffer_free")
        reduce_step = sem("reduce_step")
        var_ready = sem("var_ready")
        std_ready = sem("std_ready")
        x1_ready = sem("x1_ready")
        x1_turned = sem("x1_turned")
        x1T_copied = sem("x1T_copied")
        h_ready = sem("h_ready")
        h_saved = sem("h_saved")
        hrow_ready = sem("hrow_ready")
        act_step = sem("act_step")
        hrow_stored = [sem(f"hrow_stored{o}") for o in range(GT)]
        attend_step = sem("attend_step")
        logits_ready = sem("logits_ready")
        exp_ready = sem("exp_ready")
        neg_ready = sem("neg_ready")
        uexp_ready = sem("uexp_ready")
        y_ready = sem("y_ready")
        vars_ready = sem("vars_ready")
        stds_ready = sem("stds_ready")
        norm_step = sem("norm_step")
        rid_ready = sem("rid_ready")
        out_ready = sem("out_ready")
        flag_spread = sem("flag_spread")
        flag_checked = sem("flag_checked")
        flag_ready = sem("flag_ready")
        d_tile_loaded = sem("d_tile_loaded")
        d_chunk_loaded = [sem(f"d_chunk_loaded{b}") for b in range(2)]
        d_chunk_used = sem("d_chunk_used")
        d_chunk_step = sem("d_chunk_step")
        d_max_step = sem("d_max_step")
        d_var_ready = sem("d_var_ready")
        d_std_ready = sem("d_std_ready")
        d_x1_ready = sem("d_x1_ready")
        d_x1_turned = sem("d_x1_turned")
        d_x1T_copied = sem("d_x1T_copied")
        d_h_ready = sem("d_h_ready")
        d_h_saved = sem("d_h_saved")
        d_tile_stored = sem("d_tile_stored")
        d_rows_loaded = sem("d_rows_loaded")
        e_tile_loaded = sem("e_tile_loaded")
        e_step = sem("e_step")
        e_logits_ready = sem("e_logits_ready")
        e_exp_ready = sem("e_exp_ready")
        e_weights_ready = sem("e_weights_ready")
        e_turned = sem("e_turned")
        e_turn_copied = sem("e_turn_copied")
        e_sum_ready = sem("e_sum_ready")
        e_neg_ready = sem("e_neg_ready")
        e_uexp_ready = sem("e_uexp_ready")
        e_var_ready = sem("e_var_ready")
        e_std_ready = sem("e_std_ready")
        e_y_ready = sem("e_y_ready")
        e_out_stored = sem("e_out_stored")
        pool_passed = sem("pool_passed")
        sp_passed = sem("sp_passed")
        dve_passed = sem("dve_passed")
        out_stored = [sem(f"out_stored{o}") for o in range(GT)]

        adj_t = adj.rearrange("(t p) n -> t p n", p=P)
        x_t = x.rearrange("(t p) d -> t p d", p=P)
        x_c = x.rearrange("(c j) d -> c (j d)", j=CHUNK)
        x1_t = x1_all.rearrange("(t p) d -> t p d", p=P)
        h_t = h_all.rearrange("(t p) d -> t p d", p=P)
        d_t = d_all.rearrange("(t p) c -> t p c", p=P)
        v_t = v_all.rearrange("(t p) c -> t p c", p=P)
        out_t = out.rearrange("(t p) d -> t p d", p=P)
        x_g = x.rearrange("(q o p) d -> q p o d", o=GT, p=P)
        lists_g = lists.rearrange("(q o p) r -> q p o r", o=GT, p=P)

        block = ctx.enter_context(nc.Block())

        @block.sync
        def _(sp):
            sp.dma_start(w_aug[:, 0:D], W).then_inc(weights_loaded, 16)
            with nc.allow_non_contiguous_dma("two columns of 128"):
                sp.dma_start(a3[:, 0:1], a[D:2 * D, :]).then_inc(weights_loaded, 16)
                sp.dma_start(a3[:, 2:3], a[0:D, :]).then_inc(weights_loaded, 16)

            def group(q):
                sp.wait_ge(lists_stored, 16 * GT * q)
                sp.dma_start(rec[:, :, XCOL:REC], x_g[q]).then_inc(x_loaded, 16)
                for o in range(GT):
                    sp.wait_ge(adj_free, GT * q + o + 1)
                    sp.dma_start(adj_in[:, o % 2, :], adj_t[q * GT + o]).then_inc(adj_loaded[o % 2], 16)
                sp.wait_ge(lists_stored, 16 * GT * (q + 1))
                sp.dma_start(srt[:, bass.ds(q * GT, GT), :], lists_g[q]).then_inc(sorted_loaded, 16)

            with sp.Fori(0, GROUPS) as q:
                group(q)

            def dense():
                for o in range(GT):
                    sp.wait_ge(out_stored[o], 16 * GROUPS)
                with sp.Fori(0, TILES) as t:
                    sp.dma_start(d_adj, adj_t[t]).then_inc(d_tile_loaded, 16)
                    sp.dma_start(d_x[:, :], x_t[t]).then_inc(d_tile_loaded, 16)
                    with sp.Fori(0, CHUNKS // 2) as c:
                        for b in range(2):
                            sp.wait_ge(d_chunk_used, t * CHUNKS + c * 2 + b + 1)
                            sp.dma_start(G[:, b, 0:CHUNK * D], x_c[c * 2 + b].partition_broadcast(P)
                                         ).then_inc(d_chunk_loaded[b], 16)
                    sp.wait_ge(d_h_saved, t + 1)
                    sp.dma_start(x1_t[t], x1w[:, 0, :]).then_inc(d_tile_stored, 16)
                    sp.dma_start(h_t[t], d_h[:, 0:D]).then_inc(d_tile_stored, 16)
                    with nc.allow_non_contiguous_dma("a column of 128"):
                        sp.dma_start(d_t[t], d_h[:, D:D + 1]).then_inc(d_tile_stored, 16)
                        sp.dma_start(v_t[t], d_h[:, D + 1:D + 2]).then_inc(d_tile_stored, 16)
                    sp.wait_ge(d_tile_stored, 64 * (t + 1))
                    sp.sem_inc(sp_passed, 1)
                sp.dma_start(d_rows, d_all.rearrange("n c -> (n c)").partition_broadcast(P)).then_inc(d_rows_loaded, 16)
                sp.dma_start(v_rows, v_all.rearrange("n c -> (n c)").partition_broadcast(P)).then_inc(d_rows_loaded, 16)
                sp.dma_start(h_rows, h_all.rearrange("(t p) d -> p t d", p=P)).then_inc(d_rows_loaded, 16)
                with sp.Fori(0, TILES) as t:
                    sp.dma_start(d_adj, adj_t[t]).then_inc(e_tile_loaded, 16)
                    sp.dma_start(d_x[:, :], x1_t[t]).then_inc(e_tile_loaded, 16)
                    sp.dma_start(h_own[:, :], h_t[t]).then_inc(e_tile_loaded, 16)
                    sp.wait_ge(e_y_ready, t + 1)
                    sp.dma_start(out_t[t], yw[:, 0, :]).then_inc(e_out_stored, 16)
                    sp.wait_ge(e_out_stored, 16 * (t + 1))
                    sp.sem_inc(sp_passed, 1)

            sp.wait_ge(flag_ready, 1)
            with sp.If(sp.value_load(flag_int[0:1, 0:1], min_val=0, max_val=1) > 0):
                dense()

        @block.gpsimd
        def _(pool):
            pool.sem_inc(buffer_free, 2)
            pool.iota(ident[:, :], [[-1, P]], base=0, channel_multiplier=1,
                      allow_small_or_imprecise_dtypes=True).then_inc(consts_pool, 1)
            pool.iota(local_iota[:, :], [[1, SEGMENT]], base=1, channel_multiplier=0,
                      allow_small_or_imprecise_dtypes=True).then_inc(consts_pool, 1)
            pool.iota(seg_base[:, :], [[SEGMENT, SEGMENTS], [0, 8]], base=0, channel_multiplier=0,
                      allow_small_or_imprecise_dtypes=True).then_inc(consts_pool, 1)
            pool.iota(row_id[:, :], [[P, TILES]], base=0, channel_multiplier=1,
                      allow_small_or_imprecise_dtypes=True).then_inc(consts_pool, 1)
            pool.iota(tie[:, :], [[P, GT]], base=0, channel_multiplier=1,
                      allow_small_or_imprecise_dtypes=True).then_inc(consts_pool, 1)
            pool.iota(rank_base[:, :], [[GROWS, GROUPS], [0, GT]], base=0, channel_multiplier=0,
                      allow_small_or_imprecise_dtypes=True).then_inc(consts_pool, 1)
            pool.iota(slot_iota[:, :], [[1, LIST]], base=0, channel_multiplier=0,
                      allow_small_or_imprecise_dtypes=True).then_inc(consts_pool, 1)

            def gathers(turn, o, table, width):
                pool.wait_ge(idx_ready, GT * turn + o + 1)
                pool.wait_ge(buffer_free, GT * turn + o + 1)
                pool.sem_inc(pool_passed, 1)
                for k in range(SLOTS[o]):
                    pool.indirect_dma_start(
                        out=G[:, o % 2, k * width:(k + 1) * width], out_offset=None, in_=table,
                        in_offset=bass.IndirectOffsetOnAxis(ap=idx[:, o, k:k + 1], axis=0),
                    ).then_inc(gathered[o % 2], 16)

            def store_lists(q):
                pool.wait_ge(ranked, q + 1)
                pool.wait_ge(x_loaded, 16 * (q + 1))
                pool.sem_inc(pool_passed, 1)
                for o in range(GT):
                    pool.indirect_dma_start(
                        out=lists, out_offset=bass.IndirectOffsetOnAxis(ap=rank_u[:, o:o + 1], axis=0),
                        in_=rec[:, o, :], in_offset=None).then_inc(lists_stored, 16)

            def store_hrow(q, o):
                pool.wait_ge(hrow_ready, GT * q + o + 1)
                pool.sem_inc(pool_passed, 1)
                pool.indirect_dma_start(
                    out=htab, out_offset=bass.IndirectOffsetOnAxis(ap=rid[:, o:o + 1], axis=0),
                    in_=hrow[:, o, :], in_offset=None).then_inc(hrow_stored[o], 16)

            def store_out(q, o):
                pool.wait_ge(out_ready, GT * q + o + 1)
                pool.sem_inc(pool_passed, 1)
                pool.indirect_dma_start(
                    out=out, out_offset=bass.IndirectOffsetOnAxis(ap=rid[:, o:o + 1], axis=0),
                    in_=yw[:, o, :], in_offset=None).then_inc(out_stored[o], 16)

            def max_group(q, first=False, last=False):
                for o in range(GT):
                    gathers(q, o, x, D)
                    if not first:
                        store_hrow(q - 1, o)
                    if o == 5 and not last:
                        store_lists(q + 1)

            store_lists(0)
            max_group(0, first=True)
            with pool.Fori(1, GROUPS - 1) as q:
                max_group(q)
            max_group(GROUPS - 1, last=True)
            for o in range(GT):
                store_hrow(GROUPS - 1, o)
            for o in range(GT):
                pool.wait_ge(hrow_stored[o], 16 * GROUPS)
            for o in range(GT):
                gathers(GROUPS, o, htab, HCOLS)
            with pool.Fori(1, GROUPS) as q:
                for o in range(GT):
                    gathers(q + GROUPS, o, htab, HCOLS)
                    store_out(q - 1, o)
            for o in range(GT):
                store_out(GROUPS - 1, o)
            for o in range(GT):
                pool.wait_ge(out_stored[o], 16 * GROUPS)

        @block.scalar
        def _(act):
            act.sem_inc(adj_free, 2)

            def convert(q, o):
                t = GT * q + o
                if o == 0:
                    act.wait_ge(ranked, q)
                act.wait_ge(adj_loaded[o % 2], 16 * (GT // 2 * q + o // 2 + 1))
                act.wait_ge(adj_free, t + 2)
                act.wait_ge(keyed, t + 1)
                nc.scalar.activation(adj16[:, o % 2, :], adj_in[:, o % 2, :], ACT.Copy,
                                     accum_out=sums[:, 0, o:o + 1]).then_inc(converted, 1)
                nc.scalar.activation(squares[:, :], adj_in[:, o % 2, :], ACT.Square,
                                     accum_out=sums[:, 1, o:o + 1]).then_inc(adj_free, 1)

            def indices(turn, q, o):
                nc.scalar.copy(idx[:, o, :], srt[:, q * GT + o, 0:LIST]).then_inc(idx_ready, 1)

            def max_tile(q, o):
                t = GT * q + o
                act.wait_ge(var_ready, t + 1)
                nc.scalar.sqrt(std[:, :], mv[:, 1:2]).then_inc(std_ready, 1)
                act.wait_ge(x1_turned, t + 1)
                act.wait_ge(h_ready, t)
                nc.scalar.copy(x1T[:, :], psT[:, 0:P]).then_inc(x1T_copied, 1)
                act.wait_ge(h_ready, t + 1)
                act.wait_ge(hrow_stored[o], 16 * q)
                nc.scalar.activation(sgn[:, :], psH[:, D + 1:D + 2], ACT.Sign).then_inc(act_step, 1)
                nc.scalar.copy(hrow[:, o, 0:D + 1], psH[:, 0:D + 1]).then_inc(act_step, 1)
                nc.scalar.copy(hown[:, q * GT + o, 0:D], psH[:, 0:D]).then_inc(act_step, 1)
                nc.scalar.copy(hown[:, q * GT + o, D:D + 1], psH[:, D + 2:D + 3]).then_inc(act_step, 1)
                nc.scalar.copy(rid[:, o:o + 1], srt[:, q * GT + o, ROW:ROW + 1]).then_inc(act_step, 1)
                act.wait_ge(act_step, 5 * (t + 1))
                nc.scalar.square(hrow[:, o, D + 1:D + 2], sgn[:, :]).then_inc(hrow_ready, 1)
                act.wait_ge(hrow_ready, t + 1)
                act.sem_inc(h_saved, 1)

            def max_group(q, first=False, last=False):
                if not first:
                    for o in (6, 7):
                        indices(q, q, o)
                for o in range(GT):
                    if o < GT // 2 and not last:
                        convert(q + 1, 2 * o)
                        convert(q + 1, 2 * o + 1)
                    max_tile(q, o)
                    if o == 6:
                        if last:
                            for i in range(6):
                                indices(q + 1, 0, i)
                        else:
                            act.wait_ge(sorted_loaded, 16 * (q + 2))
                            for i in range(6):
                                indices(q + 1, q + 1, i)

            def attend_tile(q, o):
                t = GT * q + o
                act.wait_ge(logits_ready, t + 1)
                nc.scalar.activation(pe_[:, 0:SLOTS[o]], em[:, 0:SLOTS[o]], ACT.Exp, bias=nmx[:, :],
                                     accum_out=zs[:, :]).then_inc(exp_ready, 1)
                act.wait_ge(neg_ready, t + 1)
                nc.scalar.activation(uexp[:, :], uneg[:, :], ACT.Exp).then_inc(uexp_ready, 1)
                act.wait_ge(hrow_stored[o], 16 * GROUPS)
                act.wait_ge(out_stored[o], 16 * q)
                nc.scalar.copy(rid[:, o:o + 1], srt[:, q * GT + o, ROW:ROW + 1]).then_inc(rid_ready, 1)

            def attend_group(q, first=False, last=False):
                for o in (6, 7):
                    indices(q + GROUPS, q, o)
                for o in range(GT):
                    attend_tile(q, o)
                    if o == 6 and not last:
                        for i in range(6):
                            indices(q + 1 + GROUPS, q + 1, i)
                act.wait_ge(vars_ready, q + 1)
                nc.scalar.sqrt(stds[:, :], mvs[:, :, 1]).then_inc(stds_ready, 1)

            act.wait_ge(wT_ready, 1)
            nc.scalar.copy(wT[:, :], psW[:, 0:P]).then_inc(wT_copied, 1)
            act.wait_ge(wa_ready, 1)
            nc.scalar.copy(w_aug[:, D:D + 3], psW[:, P:P + 3]).then_inc(w_aug_ready, 1)

            for o in range(GT):
                convert(0, o)
            act.wait_ge(sorted_loaded, 16)
            for o in range(GT):
                indices(0, 0, o)
            max_group(0, first=True)
            with act.Fori(1, GROUPS - 1) as q:
                max_group(q)
            max_group(GROUPS - 1, last=True)
            attend_group(0)
            with act.Fori(1, GROUPS - 1) as q:
                attend_group(q)
            attend_group(GROUPS - 1, last=True)

            def dense():
                with act.Fori(0, TILES) as t:
                    act.wait_ge(d_var_ready, t + 1)
                    nc.scalar.sqrt(std[:, :], mv[:, 1:2]).then_inc(d_std_ready, 1)
                    act.wait_ge(d_x1_turned, t + 1)
                    nc.scalar.copy(x1T[:, :], psT[:, 0:P]).then_inc(d_x1T_copied, 1)
                    act.wait_ge(d_h_ready, t + 1)
                    nc.scalar.copy(d_h[:, :], psH[:, 0:D + 3]).then_inc(act_step, 1)
                    nc.scalar.activation(sgn[:, :], psH[:, D + 1:D + 2], ACT.Sign).then_inc(act_step, 1)
                    act.wait_ge(act_step, 5 * TILES + 3 * t + 2)
                    nc.scalar.copy(s_all[:, bass.ds(t, 1)], d_h[:, D + 2:D + 3]).then_inc(act_step, 1)
                    nc.scalar.square(d_h[:, D + 1:D + 2], sgn[:, :]).then_inc(d_h_saved, 1)
                with act.Fori(0, TILES) as t:
                    act.wait_ge(e_logits_ready, t + 1)
                    nc.scalar.activation(d_p, d_z, ACT.Exp, bias=nmx[:, :], accum_out=zs[:, :]
                                         ).then_inc(e_exp_ready, 1)
                    for c in range(TILES):
                        act.wait_ge(e_turned, TILES * t + c + 1)
                        nc.scalar.copy(d_wT[:, c % 2, :], psT[:, 0:P]).then_inc(e_turn_copied, 1)
                    act.wait_ge(e_neg_ready, t + 1)
                    nc.scalar.activation(uexp[:, :], uneg[:, :], ACT.Exp).then_inc(e_uexp_ready, 1)
                    act.wait_ge(e_var_ready, t + 1)
                    nc.scalar.sqrt(std[:, :], mv[:, 1:2]).then_inc(e_std_ready, 1)

            act.wait_ge(flag_ready, 1)
            with act.If(act.value_load(flag_int[0:1, 0:1], min_val=0, max_val=1) > 0):
                dense()

        @block.tensor
        def _(pe):
            pe.wait_ge(consts_dve, 4)
            pe.wait_ge(weights_loaded, 48)
            nc.tensor.transpose(psW[:, 0:P], w_aug[:, 0:D], ident[:, :]).then_inc(wT_ready, 1)
            pe.wait_ge(wT_copied, 1)
            nc.tensor.matmul(psW[:, P:P + 3], wT[:, :], a3[:, :], start=True, stop=True).then_inc(wa_ready, 1)
            pe.wait_ge(w_aug_ready, 1)

            def spread_degrees(q):
                pe.wait_ge(diag_ready, q + 1)
                for i in range(2):
                    mm = nc.tensor.matmul(psR[:, i * 512:(i + 1) * 512], ones[:, :],
                                          diag[:, 4 * i:4 * i + 4, :].rearrange("p o n -> p (o n)"),
                                          start=True, stop=True)
                mm.then_inc(degs_spread, 1)

            def max_tile(q, o):
                t = GT * q + o
                pe.wait_ge(x1_ready, t + 1)
                pe.wait_ge(x1T_copied, t)
                nc.tensor.transpose(psT[:, 0:P], x1w[:, o, :], ident[:, :]).then_inc(x1_turned, 1)
                pe.wait_ge(x1T_copied, t + 1)
                pe.wait_ge(h_saved, t)
                nc.tensor.matmul(psH[:, 0:D + 3], x1T[:, :], w_aug[:, :], start=True, stop=True).then_inc(h_ready, 1)

            spread_degrees(0)
            with pe.Fori(0, GROUPS - 1) as q:
                for o in range(GT):
                    max_tile(q, o)
                    if o == 3:
                        spread_degrees(q + 1)
            for o in range(GT):
                max_tile(GROUPS - 1, o)
            pe.wait_ge(check_step, CHECK_STEPS * GROUPS)
            nc.tensor.matmul(psW[:, 0:GT], ones[:, :], flag_sum[:, :], start=True, stop=True).then_inc(flag_spread, 1)

            def dense():
                with pe.Fori(0, TILES) as t:
                    pe.wait_ge(d_x1_ready, t + 1)
                    nc.tensor.transpose(psT[:, 0:P], x1w[:, 0, :], ident[:, :]).then_inc(d_x1_turned, 1)
                    pe.wait_ge(d_x1T_copied, t + 1)
                    nc.tensor.matmul(psH[:, 0:D + 3], x1T[:, :], w_aug[:, :], start=True, stop=True
                                     ).then_inc(d_h_ready, 1)
                pe.wait_ge(d_rows_loaded, 48)
                with pe.Fori(0, TILES) as t:
                    pe.wait_ge(e_weights_ready, t + 1)
                    for c in range(TILES):
                        pe.wait_ge(e_turn_copied, TILES * t + c)
                        nc.tensor.transpose(psT[:, 0:P], d_p[:, c * P:(c + 1) * P], ident[:, :]
                                            ).then_inc(e_turned, 1)
                        pe.wait_ge(e_turn_copied, TILES * t + c + 1)
                        mm = nc.tensor.matmul(psH[:, 0:D], d_wT[:, c % 2, :], h_rows[:, c, :],
                                              start=(c == 0), stop=(c == TILES - 1))
                    mm.then_inc(e_sum_ready, 1)

            pe.wait_ge(flag_ready, 1)
            with pe.If(pe.value_load(flag_int[0:1, 0:1], min_val=0, max_val=1) > 0):
                dense()

        @block.vector
        def _(dve):
            V = nc.vector
            dve.sem_inc(keyed, 2)
            dve.wait_ge(consts_pool, 7)
            V.tensor_scalar(ident[:, :], ident[:, :], 0.0, None, ALU.is_equal).then_inc(consts_dve, 1)
            V.memset(ones[:, :], 1.0).then_inc(consts_dve, 1)
            V.memset(a3[:, 1:2], 1.0).then_inc(consts_dve, 1)
            V.memset(flag_sum[:, :], 0.0).then_inc(consts_dve, 1)
            for o in range(GT):
                V.memset(slots_of[:, o:o + 1], float(SLOTS[o])).then_inc(consts_dve, 1)
            dve.wait_ge(consts_dve, 4 + GT)

            def extract(q, o):
                t = GT * q + o
                step = Steps(dve, extract_step, EXTRACT_STEPS, t)
                dve.wait_ge(converted, t + 1)
                seg = keys[:, :].rearrange("p (s c) -> p s c", s=SEGMENTS)
                V.tensor_tensor(seg, adj16[:, o % 2, :].rearrange("p (s c) -> p s c", s=SEGMENTS),
                                local_iota[:, :].unsqueeze(1).to_broadcast([P, SEGMENTS, SEGMENT]),
                                ALU.mult).then_inc(keyed, 1)
                dve.wait_ge(keyed, t + 3)
                dve.sem_inc(dve_passed, 1)
                for s in range(SEGMENTS):
                    mxi = V.max(cand[:, 8 * s:8 * s + 8], keys[:, s * SEGMENT:(s + 1) * SEGMENT])
                step(mxi)
                V.scalar_tensor_tensor(out=gkey[:, 1, :], in0=cand[:, :], scalar=0.0, in1=seg_base[:, :],
                                       op0=ALU.is_gt, op1=ALU.mult)
                if o == 0:
                    dve.wait_ge(lists_stored, 16 * GT * q)
                step(V.tensor_scalar(gkey[:, 0, :], cand[:, :], 0.0, 0.0, ALU.is_gt, ALU.add,
                                     accum_out=rec[:, o, DEG:DEG + 1]))
                step(V.tensor_tensor(gkey[:, 0, :], gkey[:, 1, :], cand[:, :], ALU.add), dve_passed)
                for r in range(LIST // 8):
                    step(V.max(top[:, 8 * r:8 * r + 8], gkey[:, r % 2, :]), dve_passed if r < LIST // 8 - 1 else None)
                    if r < LIST // 8 - 1:
                        step(V.match_replace(gkey[:, (r + 1) % 2, :], top[:, 8 * r:8 * r + 8],
                                             gkey[:, r % 2, :], 0.0), dve_passed)
                step(V.tensor_scalar(pad[:, :], top[:, :], 0.0, top[:, 0:1], ALU.is_equal, ALU.mult))
                step(V.tensor_tensor(pad[:, :], pad[:, :], top[:, :], ALU.add))
                step(V.tensor_scalar(rec[:, o, 0:LIST], pad[:, :], -1.0, 0.0, ALU.add, ALU.max))
                step.end()

            def sort(q):
                step = Steps(dve, sort_step, SORT_STEPS, q)
                dve.wait_ge(extract_step, EXTRACT_STEPS * GT * (q + 1))
                dve.wait_ge(adj_free, GT * (q + 1) + 2)
                degs = rec[:, :, DEG]
                V.tensor_copy(rec[:, :, ROW], row_id[:, bass.ds(q * GT, GT)])
                V.tensor_tensor(flags[:, 0, :], sums[:, 0, :], degs, ALU.not_equal)
                step(V.tensor_tensor(flags[:, 1, :], sums[:, 1, :], degs, ALU.not_equal))
                V.scalar_tensor_tensor(out=degkey[:, :], in0=degs, scalar=float(GROWS), in1=tie[:, :],
                                       op0=ALU.mult, op1=ALU.add)
                step(V.tensor_tensor(flag_sum[:, :], flag_sum[:, :], flags[:, 0, :], ALU.add))
                step(V.tensor_tensor(flag_sum[:, :], flag_sum[:, :], flags[:, 1, :], ALU.add))
                V.tensor_tensor(diag[:, :, :], ident[:, :].unsqueeze(1).to_broadcast([P, GT, P]),
                                degkey[:, :].unsqueeze(2).to_broadcast([P, GT, P]),
                                ALU.mult).then_inc(diag_ready, 1)
                dve.wait_ge(degs_spread, q + 1)
                for o in range(GT):
                    step(V.tensor_scalar(beaten[:, :], psR[:, :], degkey[:, o:o + 1], 0.0, ALU.is_gt, ALU.add,
                                         accum_out=rank[:, o:o + 1]))
                step(V.tensor_tensor(rank[:, :], rank[:, :], rank_base[:, bass.ds(q * GT, GT)], ALU.add))
                V.tensor_copy(rank_u[:, :], rank[:, :]).then_inc(ranked, 1)
                step.end()

            def check_slots(q):
                step = Steps(dve, check_step, CHECK_STEPS, q)
                dve.wait_ge(sorted_loaded, 16 * (q + 1))
                step(V.tensor_tensor(flags[:, 0, :], srt[:, bass.ds(q * GT, GT), DEG], slots_of[:, :], ALU.is_gt))
                step(V.tensor_tensor(flag_sum[:, :], flag_sum[:, :], flags[:, 0, :], ALU.add))
                step.end()

            def max_tile(q, o):
                t = GT * q + o
                K = SLOTS[o]
                step = Steps(dve, reduce_step, REDUCE_STEPS, t)
                step(V.tensor_scalar(has[:, :], srt[:, q * GT + o, DEG:DEG + 1], 1.0, None, ALU.min))
                dve.wait_ge(gathered[o % 2], 16 * (q * PER_GROUP[o % 2] + UPTO[o]))
                V.tensor_reduce(nmax[:, :], G[:, o % 2, 0:K * D].rearrange("p (k d) -> p d k", d=D),
                                AX.X, ALU.max).then_inc(buffer_free, 1)
                dve.wait_ge(buffer_free, t + 3)
                step(V.scalar_tensor_tensor(out=y0[:, :], in0=nmax[:, :], scalar=has[:, :],
                                            in1=srt[:, q * GT + o, XCOL:REC], op0=ALU.mult, op1=ALU.add))
                step(V.bn_stats(stats[:, :], y0[:, :]), dve_passed)
                step(V.bn_aggr(mv[:, :], stats[:, :]))
                V.tensor_scalar(mv[:, 1:2], mv[:, 1:2], EPS, None, ALU.add).then_inc(var_ready, 1)
                dve.wait_ge(std_ready, t + 1)
                step(V.reciprocal(rstd[:, :], std[:, :]))
                dve.wait_ge(x1_turned, GT * q)
                V.tensor_scalar(x1w[:, o, :], y0[:, :], mv[:, 0:1], rstd[:, :], ALU.subtract,
                                ALU.mult).then_inc(x1_ready, 1)
                dve.wait_ge(x1_ready, t + 1)
                step(V.tensor_copy(x1s[:, q * GT + o, :], x1w[:, o, :]))
                step.end()

            def attend_tile(q, o):
                t = GT * q + o
                K = SLOTS[o]
                own = q * GT + o
                Gt = G[:, o % 2, 0:K * HCOLS].rearrange("p (k c) -> p k c", c=HCOLS)
                dcol, vcol = Gt[:, :, D], Gt[:, :, D + 1]
                step = Steps(dve, attend_step, ATTEND_STEPS, t)
                dve.wait_ge(gathered[o % 2], 16 * ((q + GROUPS) * PER_GROUP[o % 2] + UPTO[o]))
                V.scalar_tensor_tensor(out=vm[:, 0:K], in0=slot_iota[:, 0:K], scalar=srt[:, own, DEG:DEG + 1],
                                       in1=vcol, op0=ALU.is_lt, op1=ALU.mult)
                step(V.tensor_scalar(z[:, 0:K], dcol, hown[:, own, D:D + 1], None, ALU.add))
                V.tensor_scalar(pen[:, 0:K], vm[:, 0:K], 1.0, -NEG, ALU.subtract, ALU.mult)
                step(V.scalar_tensor_tensor(out=e[:, 0:K], in0=z[:, 0:K], scalar=ALPHA, in1=z[:, 0:K],
                                            op0=ALU.mult, op1=ALU.max))
                V.reduce_sum(cnt[:, :], vm[:, 0:K], axis=AX.X)
                step(V.tensor_tensor(e[:, 0:K], e[:, 0:K], vm[:, 0:K], ALU.mult))
                step(V.tensor_tensor(em[:, 0:K], e[:, 0:K], pen[:, 0:K], ALU.add))
                step(V.reduce_max(mx[:, :], em[:, 0:K], axis=AX.X))
                V.tensor_scalar(nmx[:, :], mx[:, :], -1.0, None, ALU.mult).then_inc(logits_ready, 1)
                dve.wait_ge(exp_ready, t + 1)
                step(V.reciprocal(rz[:, :], zs[:, :]))
                step(V.scalar_tensor_tensor(out=att[:, 0:K], in0=pe_[:, 0:K], scalar=rz[:, :], in1=vm[:, 0:K],
                                            op0=ALU.mult, op1=ALU.mult))
                V.scalar_tensor_tensor(out=wgt[:, 0:K], in0=att[:, 0:K], scalar=THR, in1=att[:, 0:K],
                                       op0=ALU.is_ge, op1=ALU.mult)
                step(V.reduce_max(topa[:, :], att[:, 0:K], axis=AX.X))
                step(V.scalar_tensor_tensor(out=gate[:, :], in0=topa[:, :], scalar=THR, in1=cnt[:, :],
                                            op0=ALU.is_gt, op1=ALU.mult))
                step(V.tensor_tensor(Gt[:, :, 0:D], Gt[:, :, 0:D],
                                     wgt[:, 0:K].unsqueeze(2).to_broadcast([P, K, D]), ALU.mult))
                V.tensor_reduce(hsum[:, :], Gt[:, :, 0:D].rearrange("p k d -> p d k"), AX.X,
                                ALU.add).then_inc(buffer_free, 1)
                dve.wait_ge(buffer_free, GT * GROUPS + t + 3)
                step(V.scalar_tensor_tensor(out=u[:, :], in0=hsum[:, :], scalar=gate[:, :], in1=hown[:, own, 0:D],
                                            op0=ALU.mult, op1=ALU.add))
                V.tensor_scalar(uneg[:, :], u[:, :], 0.0, None, ALU.min).then_inc(neg_ready, 1)
                step(V.tensor_scalar(upos[:, :], u[:, :], 0.0, None, ALU.max))
                dve.wait_ge(uexp_ready, t + 1)
                step(V.scalar_tensor_tensor(out=u[:, :], in0=uexp[:, :], scalar=-1.0, in1=upos[:, :],
                                            op0=ALU.add, op1=ALU.add))
                dve.wait_ge(out_stored[o], 16 * q)
                step(V.tensor_tensor(yw[:, o, :], u[:, :], x1s[:, own, :], ALU.add))
                step(V.bn_stats(stats[:, :], yw[:, o, :]), dve_passed)
                step(V.bn_aggr(mvs[:, o, :], stats[:, :]))
                step.end()

            def norm_group(q):
                step = Steps(dve, norm_step, NORM_STEPS, q)
                dve.wait_ge(attend_step, ATTEND_STEPS * GT * (q + 1))
                step(V.tensor_scalar(mvs[:, :, 1], mvs[:, :, 1], EPS, None, ALU.add))
                dve.sem_inc(vars_ready, 1)
                dve.wait_ge(stds_ready, q + 1)
                step(V.reciprocal(rstds[:, :], stds[:, :]))
                dve.wait_ge(rid_ready, GT * (q + 1))
                for o in range(GT):
                    V.tensor_scalar(yw[:, o, :], yw[:, o, :], mvs[:, o, 0:1], rstds[:, o:o + 1], ALU.subtract,
                                    ALU.mult).then_inc(out_ready, 1)
                step.end()

            for o in range(GT):
                extract(0, o)
            sort(0)
            with dve.Fori(0, GROUPS - 1) as q:
                check_slots(q)
                for o in range(GT):
                    if o < GT // 2:
                        extract(q + 1, 2 * o)
                        extract(q + 1, 2 * o + 1)
                    max_tile(q, o)
                    if o == 3:
                        sort(q + 1)
            check_slots(GROUPS - 1)
            for o in range(GT):
                max_tile(GROUPS - 1, o)
            with dve.Fori(0, GROUPS) as q:
                for o in range(GT):
                    attend_tile(q, o)
                norm_group(q)
            dve.wait_ge(flag_spread, 1)
            V.reduce_max(flag[:, :], psW[:, 0:GT], axis=AX.X).then_inc(flag_checked, 1)
            dve.wait_ge(flag_checked, 1)
            V.tensor_scalar(flag_int[:, :], flag[:, :], 1.0, None, ALU.min).then_inc(flag_ready, 1)

            def dense_max(t):
                step = Steps(dve, d_max_step, DENSE_MAX_STEPS, t)
                dve.wait_ge(d_tile_loaded, 32 * (t + 1))
                V.tensor_scalar(d_bias, d_adj, 0.0, FMIN, ALU.is_equal, ALU.mult)
                V.memset(d_acc[:, :], FMIN)
                step(V.tensor_scalar(d_sum, d_adj, 0.0, 0.0, ALU.not_equal, ALU.add, accum_out=cnt[:, :]))
                step(V.tensor_scalar(d_has[:, :], cnt[:, :], 1.0, None, ALU.min), dve_passed)
                with dve.Fori(0, CHUNKS // 2) as c:
                    for b in range(2):
                        chunk = t * CHUNKS + c * 2 + b
                        link = Steps(dve, d_chunk_step, CHUNK_STEPS, chunk)
                        dve.wait_ge(d_chunk_loaded[b], 16 * (t * (CHUNKS // 2) + c + 1))
                        summed = d_sum.rearrange("p (j d) -> p j d", d=D)
                        V.tensor_tensor(summed, G[:, b, 0:CHUNK * D].rearrange("p (j d) -> p j d", d=D),
                                        d_bias[:, bass.ds((c * 2 + b) * CHUNK, CHUNK)].unsqueeze(2)
                                        .to_broadcast([P, CHUNK, D]), ALU.add).then_inc(d_chunk_used, 1)
                        dve.wait_ge(d_chunk_used, chunk + 3)
                        link(V.tensor_reduce(d_max[:, :], d_sum.rearrange("p (j d) -> p d j", d=D), AX.X, ALU.max))
                        link(V.tensor_tensor(d_acc[:, :], d_acc[:, :], d_max[:, :], ALU.max))
                        link.end()
                step(V.scalar_tensor_tensor(out=y0[:, :], in0=d_acc[:, :], scalar=d_has[:, :], in1=d_x[:, :],
                                            op0=ALU.mult, op1=ALU.add))
                step(V.bn_stats(stats[:, :], y0[:, :]), dve_passed)
                step(V.bn_aggr(mv[:, :], stats[:, :]))
                V.tensor_scalar(mv[:, 1:2], mv[:, 1:2], EPS, None, ALU.add).then_inc(d_var_ready, 1)
                dve.wait_ge(d_std_ready, t + 1)
                step(V.reciprocal(rstd[:, :], std[:, :]))
                V.tensor_scalar(x1w[:, 0, :], y0[:, :], mv[:, 0:1], rstd[:, :], ALU.subtract,
                                ALU.mult).then_inc(d_x1_ready, 1)
                step.end()

            def dense_attend(t):
                step = Steps(dve, e_step, DENSE_ATTEND_STEPS, t)
                dve.wait_ge(e_tile_loaded, 48 * (t + 1))
                step(V.scalar_tensor_tensor(out=d_vm, in0=d_adj, scalar=0.0, in1=v_rows, op0=ALU.is_gt, op1=ALU.mult))
                step(V.reduce_sum(cnt[:, :], d_vm, axis=AX.X))
                step(V.tensor_scalar(d_p, d_rows, s_all[:, bass.ds(t, 1)], None, ALU.add))
                step(V.scalar_tensor_tensor(out=d_z, in0=d_p, scalar=ALPHA, in1=d_p, op0=ALU.mult, op1=ALU.max))
                step(V.tensor_tensor(d_z, d_z, d_vm, ALU.mult))
                step(V.tensor_scalar(d_p, d_vm, 1.0, -NEG, ALU.subtract, ALU.mult))
                step(V.tensor_tensor(d_z, d_z, d_p, ALU.add))
                step(V.reduce_max(mx[:, :], d_z, axis=AX.X))
                V.tensor_scalar(nmx[:, :], mx[:, :], -1.0, None, ALU.mult).then_inc(e_logits_ready, 1)
                dve.wait_ge(e_exp_ready, t + 1)
                step(V.reciprocal(rz[:, :], zs[:, :]))
                step(V.scalar_tensor_tensor(out=d_z, in0=d_p, scalar=rz[:, :], in1=d_vm, op0=ALU.mult, op1=ALU.mult))
                step(V.reduce_max(topa[:, :], d_z, axis=AX.X))
                step(V.scalar_tensor_tensor(out=gate[:, :], in0=topa[:, :], scalar=THR, in1=cnt[:, :],
                                            op0=ALU.is_gt, op1=ALU.mult))
                V.scalar_tensor_tensor(out=d_p, in0=d_z, scalar=THR, in1=d_z, op0=ALU.is_ge,
                                       op1=ALU.mult).then_inc(e_weights_ready, 1)
                dve.wait_ge(e_sum_ready, t + 1)
                step(V.tensor_scalar(hsum[:, :], psH[:, 0:D], gate[:, :], None, ALU.mult))
                step(V.tensor_tensor(u[:, :], hsum[:, :], h_own[:, :], ALU.add))
                V.tensor_scalar(uneg[:, :], u[:, :], 0.0, None, ALU.min).then_inc(e_neg_ready, 1)
                step(V.tensor_scalar(upos[:, :], u[:, :], 0.0, None, ALU.max))
                dve.wait_ge(e_uexp_ready, t + 1)
                step(V.scalar_tensor_tensor(out=u[:, :], in0=uexp[:, :], scalar=-1.0, in1=upos[:, :],
                                            op0=ALU.add, op1=ALU.add))
                step(V.tensor_tensor(y0[:, :], u[:, :], d_x[:, :], ALU.add))
                step(V.bn_stats(stats[:, :], y0[:, :]), dve_passed)
                step(V.bn_aggr(mv[:, :], stats[:, :]))
                V.tensor_scalar(mv[:, 1:2], mv[:, 1:2], EPS, None, ALU.add).then_inc(e_var_ready, 1)
                dve.wait_ge(e_std_ready, t + 1)
                step(V.reciprocal(rstd[:, :], std[:, :]))
                V.tensor_scalar(yw[:, 0, :], y0[:, :], mv[:, 0:1], rstd[:, :], ALU.subtract,
                                ALU.mult).then_inc(e_y_ready, 1)
                step.end()

            def dense():
                dve.sem_inc(d_chunk_used, 2)
                for o in range(GT):
                    dve.wait_ge(out_stored[o], 16 * GROUPS)
                with dve.Fori(0, TILES) as t:
                    dense_max(t)
                dve.wait_ge(d_rows_loaded, 48)
                with dve.Fori(0, TILES) as t:
                    dense_attend(t)

            dve.wait_ge(flag_ready, 1)
            with dve.If(dve.value_load(flag_int[0:1, 0:1], min_val=0, max_val=1) > 0):
                dense()


_INS = ['x', 'adj', 'L1_gnn_W', 'L1_gnn_a']


def kernel(**inputs):
    import numpy as _np
    import concourse.bacc as _bacc
    from concourse import mybir as _mybir
    from concourse.bass_utils import run_bass_kernel_spmd as _run

    nc = _bacc.Bacc("TRN2", target_bir_lowering=False, num_devices=1)
    arrays, args = {}, []
    for name in _INS:
        a = _np.ascontiguousarray(inputs[name])
        arrays[f"in_{name}_dram"] = a
        args.append(nc.dram_tensor(f"in_{name}_dram", a.shape, _mybir.dt.from_np(a.dtype), kind="ExternalInput").ap())
    args.append(nc.dram_tensor("out_0_dram", (N, D), _mybir.dt.float32, kind="ExternalOutput").ap())
    args.append(nc.dram_tensor("lists_dram", (N, REC), _mybir.dt.float32, kind="Internal").ap())
    args.append(nc.dram_tensor("htab_dram", (N, HCOLS), _mybir.dt.float32, kind="Internal").ap())
    for name, cols in ("x1_dram", D), ("h_dram", D), ("d_dram", 1), ("v_dram", 1):
        args.append(nc.dram_tensor(name, (N, cols), _mybir.dt.float32, kind="Internal").ap())
    build(nc, *args)
    r = _run(nc, [arrays], core_ids=[0])
    return r.results[0]["out_0_dram"]
```

```python
from contextlib import ExitStack

import concourse.bass as bass
import concourse.mybir as mybir

ALU = mybir.AluOpType
ACT = mybir.ActivationFunctionType
AX = mybir.AxisListType
F32, BF16, I32, U32 = mybir.dt.float32, mybir.dt.bfloat16, mybir.dt.int32, mybir.dt.uint32

P = 128
N = 4096
D = 128
TILES = N // P
GT = 8
GROUPS = TILES // GT
GROWS = GT * P
SEGMENT = 256
SEGMENTS = N // SEGMENT
CAND = 8 * SEGMENTS
LIST = 40
DEG, ROW, XCOL = LIST, LIST + 1, LIST + 2
REC = XCOL + D
SLOTS = [36, 22, 20, 18, 17, 16, 14, 13]
HCOLS = D + 1
GBUF = max(SLOTS) * D
PAIRS = GT // 2
QUARTERS = 8
QC = N // QUARTERS
EXTRACTS = [2, 2, 1, 1, 1, 1, 0, 0]
FIRST = [sum(EXTRACTS[:o]) for o in range(GT)]
CONVERTED = [min(FIRST[o] + EXTRACTS[o] + 2, GT) for o in range(GT)]
EPS, THR, ALPHA, NEG = 1e-5, 1e-4, 0.2, -1e9
FAR = NEG / ALPHA
FMIN = -3.4028234663852886e38

UPTO = [sum(SLOTS[i] for i in range(o % 2, o + 1, 2)) for o in range(GT)]
PER_GROUP = [UPTO[GT - 2], UPTO[GT - 1]]
UPTO1 = [sum(SLOTS[PAIRS + j] for j in range(i % 2, i + 1, 2)) for i in range(PAIRS)]
PER_GROUP1 = [UPTO1[PAIRS - 2], UPTO1[PAIRS - 1]]

EXTRACT_STEPS = 11
SORT_STEPS = 8
CHECK_STEPS = 2
REDUCE_STEPS = 4
NORM_TILE_STEPS = 2
CHUNK = 32
CHUNKS = N // CHUNK
CHUNK_STEPS = 2
DENSE_MAX_STEPS = 6
DENSE_ATTEND_STEPS = 20
SPARSE_STEPS = 5
SHIFT_STEPS = 3
PAIR_STEPS = 18
NORM_STEPS = 2


class Steps:

    def __init__(self, eng, sem, per, turn):
        self.eng, self.sem, self.per, self.base, self.k = eng, sem, per, turn * per, 0

    def __call__(self, instruction, passed=None):
        self.k += 1
        instruction.then_inc(self.sem, 1)
        self.eng.wait_ge(self.sem, self.base + self.k)
        if passed is not None:
            self.eng.sem_inc(passed, 1)

    def end(self):
        assert self.k == self.per, (self.k, self.per)


def build(nc, x, adj, W, a, out, lists, htab, x1_all, h_all, d_all, v_all):
    with ExitStack() as ctx:
        def sb(name, shape, dt=F32):
            return ctx.enter_context(nc.sbuf_tensor(name, shape, dt))

        def ps(name, shape):
            return ctx.enter_context(nc.psum_tensor(name, shape, F32))

        def sem(name):
            return ctx.enter_context(nc.semaphore(name))

        ident = sb("ident", [P, P])
        ones = sb("ones", [P, P])
        local_iota = sb("local_iota", [P, SEGMENT], BF16)
        seg_base = sb("seg_base", [P, CAND])
        row_id = sb("row_id", [P, TILES])
        tie = sb("tie", [P, GT])
        rank_base = sb("rank_base", [P, TILES])
        slot_iota = sb("slot_iota", [P, LIST])
        slots_of = sb("slots_of", [P, GT])
        w_aug = sb("w_aug", [P, D + 3])
        wT = sb("wT", [P, D])
        a3 = sb("a3", [P, 3])
        adj_in = sb("adj_in", [P, 2, N], I32)
        adj16 = sb("adj16", [P, 2, N], BF16)
        scratch16 = sb("scratch16", [P, 2, N], BF16)
        squares, keys = scratch16[:, 0, :], scratch16[:, 1, :]
        sums = sb("sums", [P, 2, GT])
        cand = sb("cand", [P, 2, CAND])
        gkey = sb("gkey", [P, 2, CAND])
        listed = sb("listed", [P, GT, LIST])
        filled = sb("filled", [P, GT, LIST])
        flags = sb("flags", [P, 2, GT])
        flag_sum = sb("flag_sum", [P, GT])
        rec = sb("rec", [P, GT, REC])
        degkey = sb("degkey", [P, GT])
        diag = sb("diag", [P, GT, P])
        negkey = sb("negkey", [P, GT])
        beaten = sb("beaten", [P, GROWS], BF16)
        rank = sb("rank", [P, GT])
        rank_u = sb("rank_u", [P, GT], U32)
        srt = sb("srt", [P, TILES, XCOL])
        own = sb("own", [P, TILES, D])
        idx = sb("idx", [P, GT, LIST], U32)
        rid = sb("rid", [P, GT], U32)
        G = sb("G", [P, 2, GBUF])
        nmax = sb("nmax", [P, D])
        has = sb("has", [P, 1])
        y0 = sb("y0", [P, D])
        stats = sb("stats", [P, 6])
        mv = sb("mv", [P, 2])
        std = sb("std", [P, 1])
        rstd = sb("rstd", [P, 1])
        x1w = sb("x1w", [P, GT, D])
        x1T = sb("x1T", [P, P])
        hown = sb("hown", [P, TILES, D + 1])
        hrow = sb("hrow", [P, GT, HCOLS])
        v_own = sb("v_own", [P, TILES])
        sgn = sb("sgn", [P, 1])
        z = sb("z", [P, LIST])
        e = sb("e", [P, LIST])
        pen = sb("pen", [P, LIST])
        em = sb("em", [P, LIST])
        mx = sb("mx", [P, 2])
        nmx = sb("nmx", [P, 1])
        zmax = sb("zmax", [P, 1])
        emax = sb("emax", [P, 1])
        shift = sb("shift", [P, 2])
        p_exp = sb("p_exp", [P, LIST])
        zs = sb("zs", [P, 2])
        rz = sb("rz", [P, 2])
        thz = sb("thz", [P, 1])
        gate = sb("gate", [P, 2])
        least = sb("least", [P, 1])
        att = sb("att", [P, LIST])
        wgt = sb("wgt", [P, LIST])
        hsum = sb("hsum", [P, D])
        u = sb("u", [P, 2, D])
        upos = sb("upos", [P, 2, D])
        uneg = sb("uneg", [P, 2, D])
        uexp = sb("uexp", [P, 2, D])
        adj_rid = sb("adj_rid", [P, PAIRS], U32)
        h_nat = sb("h_nat", [P, TILES, HCOLS])
        d_bc = sb("d_bc", [P, N])
        wTs = diag[:, :, :].rearrange("p o n -> p (o n)").rearrange("p (b n) -> p b n", b=2)
        dense_w = [adj16[:, :, :].rearrange("p b n -> p (b n)").bitcast(F32),
                   scratch16[:, :, :].rearrange("p b n -> p (b n)").bitcast(F32)]
        yw = x1w
        mvs = sb("mvs", [P, GT, 2])
        stds = sb("stds", [P, GT])
        rstds = sb("rstds", [P, GT])

        flag = sb("flag", [P, 1])
        flag_int = sb("flag_int", [P, 1], I32)
        s_all = sb("s_all", [P, TILES])
        topa = sb("topa", [P, 1])
        cnt = sb("cnt", [P, 1])
        d_has = sb("d_has", [P, 1])
        d_acc, d_max, d_x, h_own = (rows[:, 1, :] for rows in (u, upos, uneg, uexp))
        d_h = sb("d_h", [P, D + 3])
        d_wT = wTs[:, :, 0:P]
        d_adj = adj_in[:, 0, :]
        d_bias, d_sum = d_bc[:, :], own[:, :, :].rearrange("p t d -> p (t d)")
        d_z, d_vm = dense_w[0], d_sum
        d_p = adj_in[:, 1, :].bitcast(F32)
        d_rows, v_rows = d_bc[:, :], dense_w[1]
        h_rows = G[:, 0, 0:N].rearrange("p (t d) -> p t d", d=D)

        psR = ps("psR", [P, GROWS])
        psT = ps("psT", [P, 512])
        psH = ps("psH", [P, 512])
        psW = ps("psW", [P, 512])
        psA = ps("psA", [P, 512])

        consts_pool = sem("consts_pool")
        consts_dve = sem("consts_dve")
        weights_loaded = sem("weights_loaded")
        wT_ready = sem("wT_ready")
        wT_copied = sem("wT_copied")
        wa_ready = sem("wa_ready")
        w_aug_ready = sem("w_aug_ready")
        adj_loaded = [sem(f"adj_loaded{b}") for b in range(2)]
        x_loaded = sem("x_loaded")
        adj_free = sem("adj_free")
        converted = sem("converted")
        keyed = sem("keyed")
        found = sem("found")
        extract_step = sem("extract_step")
        sort_step = sem("sort_step")
        rank_step = sem("rank_step")
        check_step = sem("check_step")
        diag_ready = sem("diag_ready")
        degs_spread = sem("degs_spread")
        ranked = sem("ranked")
        lists_stored = sem("lists_stored")
        sorted_loaded = sem("sorted_loaded")
        own_loaded = sem("own_loaded")
        idx_ready = sem("idx_ready")
        gathered = [sem(f"gathered{b}") for b in range(2)]
        buffer_free = sem("buffer_free")
        reduce_step = sem("reduce_step")
        var_ready = sem("var_ready")
        norm_tile_step = sem("norm_tile_step")
        std_ready = sem("std_ready")
        x1_ready = sem("x1_ready")
        x1_turned = sem("x1_turned")
        x1T_copied = sem("x1T_copied")
        h_ready = sem("h_ready")
        h_saved = sem("h_saved")
        hrow_ready = sem("hrow_ready")
        act_step = sem("act_step")
        hrow_stored = [sem(f"hrow_stored{o}") for o in range(GT)]
        v_checked = sem("v_checked")
        idx1_ready = sem("idx1_ready")
        gathered1 = [sem(f"gathered1_{b}") for b in range(2)]
        buffer_free1 = sem("buffer_free1")
        adj_rid_ready = sem("adj_rid_ready")
        rows_gathered = [sem(f"rows_gathered{b}") for b in range(2)]
        h_nat_loaded = sem("h_nat_loaded")
        d_diag_ready = sem("d_diag_ready")
        d_spread = sem("d_spread")
        d_bc_copied = sem("d_bc_copied")
        mask_ready = sem("mask_ready")
        shift_step = sem("shift_step")
        dense_logits_ready = sem("dense_logits_ready")
        dense_exp_ready = sem("dense_exp_ready")
        merged = sem("merged")
        dense_weights_ready = sem("dense_weights_ready")
        w_turned = sem("w_turned")
        w_turn_copied = sem("w_turn_copied")
        w_used = sem("w_used")
        sparse_step = sem("sparse_step")
        pair_step = sem("pair_step")
        logits_ready = sem("logits_ready")
        exp_ready = sem("exp_ready")
        neg_ready = sem("neg_ready")
        uexp_ready = sem("uexp_ready")
        vars_ready = sem("vars_ready")
        stds_ready = sem("stds_ready")
        norm_step = sem("norm_step")
        rid_ready = sem("rid_ready")
        out_ready = sem("out_ready")
        flag_spread = sem("flag_spread")
        flag_checked = sem("flag_checked")
        flag_ready = sem("flag_ready")
        d_tile_loaded = sem("d_tile_loaded")
        d_chunk_loaded = [sem(f"d_chunk_loaded{b}") for b in range(2)]
        d_chunk_used = sem("d_chunk_used")
        d_chunk_step = sem("d_chunk_step")
        d_max_step = sem("d_max_step")
        d_var_ready = sem("d_var_ready")
        d_std_ready = sem("d_std_ready")
        d_x1_ready = sem("d_x1_ready")
        d_x1_turned = sem("d_x1_turned")
        d_x1T_copied = sem("d_x1T_copied")
        d_h_ready = sem("d_h_ready")
        d_h_saved = sem("d_h_saved")
        d_tile_stored = sem("d_tile_stored")
        d_rows_loaded = sem("d_rows_loaded")
        e_tile_loaded = sem("e_tile_loaded")
        e_step = sem("e_step")
        e_logits_ready = sem("e_logits_ready")
        e_exp_ready = sem("e_exp_ready")
        e_weights_ready = sem("e_weights_ready")
        e_turned = sem("e_turned")
        e_turn_copied = sem("e_turn_copied")
        e_sum_ready = sem("e_sum_ready")
        e_neg_ready = sem("e_neg_ready")
        e_uexp_ready = sem("e_uexp_ready")
        e_var_ready = sem("e_var_ready")
        e_std_ready = sem("e_std_ready")
        e_y_ready = sem("e_y_ready")
        e_out_stored = sem("e_out_stored")
        pool_passed = sem("pool_passed")
        sp_passed = sem("sp_passed")
        dve_passed = sem("dve_passed")
        out_stored = [sem(f"out_stored{o}") for o in range(GT)]

        adj_t = adj.rearrange("(t p) n -> t p n", p=P)
        x_t = x.rearrange("(t p) d -> t p d", p=P)
        x_c = x.rearrange("(c j) d -> c (j d)", j=CHUNK)
        x1_t = x1_all.rearrange("(t p) d -> t p d", p=P)
        h_t = h_all.rearrange("(t p) d -> t p d", p=P)
        d_t = d_all.rearrange("(t p) c -> t p c", p=P)
        v_t = v_all.rearrange("(t p) c -> t p c", p=P)
        out_t = out.rearrange("(t p) d -> t p d", p=P)
        x_g = x.rearrange("(q o p) d -> q p o d", o=GT, p=P)
        lists_g = lists.rearrange("(q o p) r -> q p o r", o=GT, p=P)

        def tile_of(o):
            return o // 2 if o % 2 else PAIRS + o // 2

        block = ctx.enter_context(nc.Block())

        @block.sync
        def _(sp):
            sp.dma_start(w_aug[:, 0:D], W).then_inc(weights_loaded, 16)
            with nc.allow_non_contiguous_dma("two columns of 128"):
                sp.dma_start(a3[:, 0:1], a[D:2 * D, :]).then_inc(weights_loaded, 16)
                sp.dma_start(a3[:, 2:3], a[0:D, :]).then_inc(weights_loaded, 16)

            def group(q):
                sp.wait_ge(lists_stored, 16 * GT * q)
                sp.dma_start(rec[:, :, XCOL:REC], x_g[q]).then_inc(x_loaded, 16)
                for o in range(GT):
                    sp.wait_ge(adj_free, GT * q + o + 1)
                    sp.dma_start(adj_in[:, o % 2, :], adj_t[q * GT + o]).then_inc(adj_loaded[o % 2], 16)
                sp.wait_ge(lists_stored, 16 * GT * (q + 1))
                sp.dma_start(srt[:, bass.ds(q * GT, GT), :], lists_g[q][:, :, 0:XCOL]).then_inc(sorted_loaded, 16)
                sp.dma_start(own[:, bass.ds(q * GT, GT), :], lists_g[q][:, :, XCOL:REC]).then_inc(own_loaded, 16)

            with sp.Fori(0, GROUPS) as q:
                group(q)
            for o in range(GT):
                sp.wait_ge(hrow_stored[o], 16 * GROUPS)
            sp.dma_start(h_nat[:, :, :], htab.rearrange("(t p) c -> p t c", p=P)).then_inc(h_nat_loaded, 16)

            def dense():
                for o in range(GT):
                    sp.wait_ge(out_stored[o], 16 * GROUPS)
                with sp.Fori(0, TILES) as t:
                    sp.dma_start(d_adj, adj_t[t]).then_inc(d_tile_loaded, 16)
                    sp.dma_start(d_x[:, :], x_t[t]).then_inc(d_tile_loaded, 16)
                    with sp.Fori(0, CHUNKS // 2) as c:
                        for b in range(2):
                            sp.wait_ge(d_chunk_used, t * CHUNKS + c * 2 + b + 1)
                            sp.dma_start(G[:, b, 0:CHUNK * D], x_c[c * 2 + b].partition_broadcast(P)
                                         ).then_inc(d_chunk_loaded[b], 16)
                    sp.wait_ge(d_h_saved, t + 1)
                    sp.dma_start(x1_t[t], x1w[:, 0, :]).then_inc(d_tile_stored, 16)
                    sp.dma_start(h_t[t], d_h[:, 0:D]).then_inc(d_tile_stored, 16)
                    with nc.allow_non_contiguous_dma("a column of 128"):
                        sp.dma_start(d_t[t], d_h[:, D:D + 1]).then_inc(d_tile_stored, 16)
                        sp.dma_start(v_t[t], d_h[:, D + 1:D + 2]).then_inc(d_tile_stored, 16)
                    sp.wait_ge(d_tile_stored, 64 * (t + 1))
                    sp.sem_inc(sp_passed, 1)
                sp.dma_start(d_rows, d_all.rearrange("n c -> (n c)").partition_broadcast(P)).then_inc(d_rows_loaded, 16)
                sp.dma_start(v_rows, v_all.rearrange("n c -> (n c)").partition_broadcast(P)).then_inc(d_rows_loaded, 16)
                sp.dma_start(h_rows, h_all.rearrange("(t p) d -> p t d", p=P)).then_inc(d_rows_loaded, 16)
                with sp.Fori(0, TILES) as t:
                    sp.dma_start(d_adj, adj_t[t]).then_inc(e_tile_loaded, 16)
                    sp.dma_start(d_x[:, :], x1_t[t]).then_inc(e_tile_loaded, 16)
                    sp.dma_start(h_own[:, :], h_t[t]).then_inc(e_tile_loaded, 16)
                    sp.wait_ge(e_y_ready, t + 1)
                    sp.dma_start(out_t[t], yw[:, 0, :]).then_inc(e_out_stored, 16)
                    sp.wait_ge(e_out_stored, 16 * (t + 1))
                    sp.sem_inc(sp_passed, 1)

            sp.wait_ge(flag_ready, 1)
            with sp.If(sp.value_load(flag_int[0:1, 0:1], min_val=0, max_val=1) > 0):
                dense()

        @block.gpsimd
        def _(pool):
            pool.sem_inc(buffer_free, 2)
            pool.sem_inc(buffer_free1, 2)
            pool.iota(ident[:, :], [[-1, P]], base=0, channel_multiplier=1,
                      allow_small_or_imprecise_dtypes=True).then_inc(consts_pool, 1)
            pool.iota(local_iota[:, :], [[1, SEGMENT]], base=1, channel_multiplier=0,
                      allow_small_or_imprecise_dtypes=True).then_inc(consts_pool, 1)
            pool.iota(seg_base[:, :], [[SEGMENT, SEGMENTS], [0, 8]], base=0, channel_multiplier=0,
                      allow_small_or_imprecise_dtypes=True).then_inc(consts_pool, 1)
            pool.iota(row_id[:, :], [[P, TILES]], base=0, channel_multiplier=1,
                      allow_small_or_imprecise_dtypes=True).then_inc(consts_pool, 1)
            pool.iota(tie[:, :], [[P, GT]], base=0, channel_multiplier=1,
                      allow_small_or_imprecise_dtypes=True).then_inc(consts_pool, 1)
            pool.iota(rank_base[:, :], [[GROWS, GROUPS], [0, GT]], base=0, channel_multiplier=0,
                      allow_small_or_imprecise_dtypes=True).then_inc(consts_pool, 1)
            pool.iota(slot_iota[:, :], [[1, LIST]], base=0, channel_multiplier=0,
                      allow_small_or_imprecise_dtypes=True).then_inc(consts_pool, 1)

            def gathers(turn, o, table, width):
                pool.wait_ge(idx_ready, GT * turn + o + 1)
                pool.wait_ge(buffer_free, GT * turn + o + 1)
                pool.sem_inc(pool_passed, 1)
                for k in range(SLOTS[o]):
                    pool.indirect_dma_start(
                        out=G[:, o % 2, k * width:(k + 1) * width], out_offset=None, in_=table,
                        in_offset=bass.IndirectOffsetOnAxis(ap=idx[:, o, k:k + 1], axis=0),
                    ).then_inc(gathered[o % 2], 16)

            def store_lists(q):
                pool.wait_ge(ranked, q + 1)
                pool.wait_ge(sort_step, SORT_STEPS * (q + 1))
                pool.wait_ge(x_loaded, 16 * (q + 1))
                pool.sem_inc(pool_passed, 1)
                for o in range(GT):
                    pool.indirect_dma_start(
                        out=lists, out_offset=bass.IndirectOffsetOnAxis(ap=rank_u[:, o:o + 1], axis=0),
                        in_=rec[:, o, :], in_offset=None).then_inc(lists_stored, 16)

            def store_hrow(q, o):
                pool.wait_ge(hrow_ready, GT * q + o + 1)
                pool.sem_inc(pool_passed, 1)
                pool.indirect_dma_start(
                    out=htab, out_offset=bass.IndirectOffsetOnAxis(ap=rid[:, o:o + 1], axis=0),
                    in_=hrow[:, o, :], in_offset=None).then_inc(hrow_stored[o], 16)

            def store_out(q, o):
                pool.wait_ge(out_ready, GT * q + o + 1)
                pool.sem_inc(pool_passed, 1)
                pool.indirect_dma_start(
                    out=out, out_offset=bass.IndirectOffsetOnAxis(ap=rid[:, o:o + 1], axis=0),
                    in_=yw[:, o, :], in_offset=None).then_inc(out_stored[o], 16)

            def max_group(q, first=False, last=False):
                for o in range(GT):
                    gathers(q, o, x, D)
                    if not first:
                        store_hrow(q - 1, o)
                    if last and o >= 2:
                        store_hrow(q, o - 2)
                    if o == 6 and not last:
                        store_lists(q + 1)

            store_lists(0)
            max_group(0, first=True)
            with pool.Fori(1, GROUPS - 1) as q:
                max_group(q)
            max_group(GROUPS - 1, last=True)
            for o in (GT - 2, GT - 1):
                store_hrow(GROUPS - 1, o)

            def gather_adj(q, i, merged_before=True):
                n = PAIRS * q + i
                pool.wait_ge(adj_rid_ready, n + 1)
                if merged_before:
                    pool.wait_ge(merged, n - 1)
                pool.sem_inc(pool_passed, 1)
                pool.indirect_dma_start(
                    out=adj_in[:, i % 2, :], out_offset=None, in_=adj,
                    in_offset=bass.IndirectOffsetOnAxis(ap=adj_rid[:, i:i + 1], axis=0),
                ).then_inc(rows_gathered[i % 2], 16)

            def gather_h(q, i, between=None):
                n = PAIRS * q + i
                pool.wait_ge(idx1_ready, n + 1)
                pool.wait_ge(buffer_free1, n + 1)
                pool.sem_inc(pool_passed, 1)
                K = SLOTS[PAIRS + i]
                for k in range(K):
                    if between and k == K // 2:
                        between()
                    pool.indirect_dma_start(
                        out=G[:, i % 2, k * HCOLS:(k + 1) * HCOLS], out_offset=None, in_=htab,
                        in_offset=bass.IndirectOffsetOnAxis(ap=idx[:, PAIRS + i, k:k + 1], axis=0),
                    ).then_inc(gathered1[i % 2], 16)

            def attend_group(q, first=False, last=False):
                for i in range(PAIRS):
                    q1, i1 = (q, i + 1) if i + 1 < PAIRS else (q + 1, 0)
                    q2, i2 = (q, i + 2) if i + 2 < PAIRS else (q + 1, i + 2 - PAIRS)
                    if not (last and i + 1 == PAIRS):
                        gather_h(q1, i1, (lambda: gather_adj(q2, i2)) if not (last and i + 2 >= PAIRS) else None)
                    if not first:
                        store_out(q - 1, 2 * i)
                        store_out(q - 1, 2 * i + 1)

            pool.wait_ge(adj_free, TILES + 2)
            gather_adj(0, 0, merged_before=False)
            gather_adj(0, 1, merged_before=False)
            for o in range(GT):
                pool.wait_ge(hrow_stored[o], 16 * GROUPS)
            gather_h(0, 0)
            attend_group(0, first=True)
            with pool.Fori(1, GROUPS - 1) as q:
                attend_group(q)
            attend_group(GROUPS - 1, last=True)
            for o in range(GT):
                store_out(GROUPS - 1, o)
            for o in range(GT):
                pool.wait_ge(out_stored[o], 16 * GROUPS)

        @block.scalar
        def _(act):
            act.sem_inc(adj_free, 2)

            def convert(q, o):
                t = GT * q + o
                if o == 0:
                    act.wait_ge(sort_step, SORT_STEPS * q)
                act.wait_ge(adj_loaded[o % 2], 16 * (GT // 2 * q + o // 2 + 1))
                act.wait_ge(adj_free, t + 2)
                act.wait_ge(keyed, t + 1)
                nc.scalar.activation(adj16[:, o % 2, :], adj_in[:, o % 2, :], ACT.Copy,
                                     accum_out=sums[:, 0, o:o + 1]).then_inc(converted, 1)
                nc.scalar.activation(squares, adj_in[:, o % 2, :], ACT.Square,
                                     accum_out=sums[:, 1, o:o + 1]).then_inc(adj_free, 1)

            def indices(turn, q, o):
                nc.scalar.copy(idx[:, o, :], srt[:, q * GT + o, 0:LIST]).then_inc(idx_ready, 1)

            def rank_rows(q):
                act.wait_ge(degs_spread, q + 1)
                act.wait_ge(lists_stored, 16 * GT * q)
                for o in range(GT):
                    nc.scalar.activation(beaten[:, :], psR[:, :], ACT.Sign, bias=negkey[:, o:o + 1],
                                         accum_out=rank[:, o:o + 1]).then_inc(rank_step, 1)
                    act.wait_ge(rank_step, GT * q + o + 1)
                nc.scalar.activation(rank_u[:, :], rank[:, :], ACT.Identity, scale=0.5,
                                     bias=rank_base[:, bass.ds(q * GT, 1)]).then_inc(ranked, 1)

            def deviation(q, o):
                act.wait_ge(var_ready, GT * q + o + 1)
                nc.scalar.sqrt(std[:, :], mv[:, 1:2]).then_inc(std_ready, 1)

            def h_tile(q, o):
                t = GT * q + o
                act.wait_ge(x1_turned, t + 1)
                act.wait_ge(h_ready, t)
                nc.scalar.copy(x1T[:, :], psT[:, 0:P]).then_inc(x1T_copied, 1)
                act.wait_ge(h_ready, t + 1)
                act.wait_ge(hrow_stored[o], 16 * q)
                nc.scalar.activation(sgn[:, :], psH[:, D + 1:D + 2], ACT.Sign).then_inc(act_step, 1)
                nc.scalar.copy(hrow[:, o, 0:D + 1], psH[:, 0:D + 1]).then_inc(act_step, 1)
                nc.scalar.copy(hown[:, q * GT + o, 0:D], psH[:, 0:D]).then_inc(act_step, 1)
                nc.scalar.copy(hown[:, q * GT + o, D:D + 1], psH[:, D + 2:D + 3]).then_inc(act_step, 1)
                nc.scalar.copy(rid[:, o:o + 1], srt[:, q * GT + o, ROW:ROW + 1]).then_inc(act_step, 1)
                act.wait_ge(act_step, 5 * (t + 1))
                nc.scalar.square(v_own[:, bass.ds(t, 1)], sgn[:, :]).then_inc(hrow_ready, 1)
                act.wait_ge(hrow_ready, t + 1)
                act.sem_inc(h_saved, 1)

            def max_group(q, first=False, last=False):
                if not first:
                    for o in (6, 7):
                        indices(q, q, o)
                for o in range(GT):
                    if not last:
                        for i in range(CONVERTED[o - 1] if o else 0, CONVERTED[o]):
                            convert(q + 1, i)
                    if o and not last:
                        h_tile(q, o - 1)
                    deviation(q, o)
                    if last or o == GT - 1:
                        h_tile(q, o)
                    if o == 5 and not last:
                        rank_rows(q + 1)
                    if o == 6:
                        if not last:
                            act.wait_ge(sorted_loaded, 16 * (q + 2))
                            for i in range(6):
                                indices(q + 1, q + 1, i)

            def mask(q, i):
                b = i % 2
                act.wait_ge(rows_gathered[b], 16 * (PAIRS // 2 * q + i // 2 + 1))
                nc.scalar.activation(adj_in[:, b, :].bitcast(F32), adj_in[:, b, :], ACT.Copy, bias=FAR,
                                     scale=-FAR).then_inc(mask_ready, 1)

            def exponentials(q, i):
                n, b = PAIRS * q + i, i % 2
                act.wait_ge(dense_logits_ready, n + 1)
                act.wait_ge(w_turned, QUARTERS * n)
                masked = adj_in[:, b, :].bitcast(F32)
                nc.scalar.activation(dense_w[b], masked, ACT.Exp, bias=shift[:, 0:1]).then_inc(dense_exp_ready, 1)
                nc.scalar.activation(masked, masked, ACT.Exp, bias=shift[:, 1:2], scale=ALPHA
                                     ).then_inc(dense_exp_ready, 1)

            def pair(q, i, last):
                n = PAIRS * q + i
                if not (last and i + 1 == PAIRS):
                    exponentials(*((q, i + 1) if i + 1 < PAIRS else (q + 1, 0)))
                act.wait_ge(logits_ready, n + 1)
                K = SLOTS[PAIRS + i]
                nc.scalar.activation(p_exp[:, 0:K], em[:, 0:K], ACT.Exp, bias=nmx[:, :],
                                     accum_out=zs[:, 0:1]).then_inc(exp_ready, 1)
                if not last:
                    nc.scalar.copy(idx[:, PAIRS + i, :], srt[:, GT * q + (GT + PAIRS + i), 0:LIST]).then_inc(idx1_ready, 1)
                    nc.scalar.copy(adj_rid[:, i:i + 1], srt[:, GT * q + (GT + i), ROW:ROW + 1]).then_inc(adj_rid_ready, 1)
                for c in range(QUARTERS):
                    if c == 5 and not (last and i + 2 >= PAIRS):
                        mask(*((q, i + 2) if i + 2 < PAIRS else (q + 1, i + 2 - PAIRS)))
                    act.wait_ge(w_turned, QUARTERS * (n + 1) + c + 1)
                    act.wait_ge(w_used, QUARTERS * n + c + 1)
                    nc.scalar.copy(wTs[:, c % 2, :], psR[:, (c % 2) * QC:(c % 2 + 1) * QC]).then_inc(w_turn_copied, 1)
                act.wait_ge(neg_ready, n + 1)
                nc.scalar.activation(uexp[:, :, :], uneg[:, :, :], ACT.Exp).then_inc(uexp_ready, 1)
                for o in (2 * i, 2 * i + 1):
                    act.wait_ge(hrow_stored[o], 16 * GROUPS)
                    act.wait_ge(out_stored[o], 16 * q)
                    nc.scalar.copy(rid[:, o:o + 1], srt[:, q * GT + tile_of(o), ROW:ROW + 1]).then_inc(rid_ready, 1)

            def attend_group(q, last=False):
                for i in range(PAIRS):
                    pair(q, i, last)
                act.wait_ge(vars_ready, q + 1)
                nc.scalar.sqrt(stds[:, :], mvs[:, :, 1]).then_inc(stds_ready, 1)

            act.wait_ge(wT_ready, 1)
            nc.scalar.copy(wT[:, :], psW[:, 0:P]).then_inc(wT_copied, 1)
            act.wait_ge(wa_ready, 1)
            nc.scalar.copy(w_aug[:, D:D + 3], psW[:, P:P + 3]).then_inc(w_aug_ready, 1)

            for o in range(GT):
                convert(0, o)
            rank_rows(0)
            act.wait_ge(sorted_loaded, 16)
            for o in range(GT):
                indices(0, 0, o)
            max_group(0, first=True)
            with act.Fori(1, GROUPS - 1) as q:
                max_group(q)
            max_group(GROUPS - 1, last=True)
            for i in range(PAIRS):
                nc.scalar.copy(adj_rid[:, i:i + 1], srt[:, i, ROW:ROW + 1]).then_inc(adj_rid_ready, 1)
            for i in range(PAIRS):
                nc.scalar.copy(idx[:, PAIRS + i, :], srt[:, PAIRS + i, 0:LIST]).then_inc(idx1_ready, 1)
            for c in range(QUARTERS):
                act.wait_ge(d_spread, c + 1)
                nc.scalar.copy(d_bc[:, c * QC:(c + 1) * QC], psR[:, (c % 2) * QC:(c % 2 + 1) * QC]
                               ).then_inc(d_bc_copied, 1)
            act.wait_ge(d_bc_copied, QUARTERS)
            act.wait_ge(keyed, TILES + 2)
            mask(0, 0)
            mask(0, 1)
            exponentials(0, 0)
            with act.Fori(0, GROUPS - 1) as q:
                attend_group(q)
            attend_group(GROUPS - 1, last=True)

            def dense():
                with act.Fori(0, TILES) as t:
                    act.wait_ge(d_var_ready, t + 1)
                    nc.scalar.sqrt(std[:, :], mv[:, 1:2]).then_inc(d_std_ready, 1)
                    act.wait_ge(d_x1_turned, t + 1)
                    nc.scalar.copy(x1T[:, :], psT[:, 0:P]).then_inc(d_x1T_copied, 1)
                    act.wait_ge(d_h_ready, t + 1)
                    nc.scalar.copy(d_h[:, :], psH[:, 0:D + 3]).then_inc(act_step, 1)
                    nc.scalar.activation(sgn[:, :], psH[:, D + 1:D + 2], ACT.Sign).then_inc(act_step, 1)
                    act.wait_ge(act_step, 5 * TILES + 3 * t + 2)
                    nc.scalar.copy(s_all[:, bass.ds(t, 1)], d_h[:, D + 2:D + 3]).then_inc(act_step, 1)
                    nc.scalar.square(d_h[:, D + 1:D + 2], sgn[:, :]).then_inc(d_h_saved, 1)
                with act.Fori(0, TILES) as t:
                    act.wait_ge(e_logits_ready, t + 1)
                    nc.scalar.activation(d_p, d_z, ACT.Exp, bias=nmx[:, :], accum_out=zs[:, 0:1]
                                         ).then_inc(e_exp_ready, 1)
                    for c in range(TILES):
                        act.wait_ge(e_turned, TILES * t + c + 1)
                        nc.scalar.copy(d_wT[:, c % 2, :], psT[:, 0:P]).then_inc(e_turn_copied, 1)
                    act.wait_ge(e_neg_ready, t + 1)
                    nc.scalar.activation(uexp[:, 0, :], uneg[:, 0, :], ACT.Exp).then_inc(e_uexp_ready, 1)
                    act.wait_ge(e_var_ready, t + 1)
                    nc.scalar.sqrt(std[:, :], mv[:, 1:2]).then_inc(e_std_ready, 1)

            act.wait_ge(flag_ready, 1)
            with act.If(act.value_load(flag_int[0:1, 0:1], min_val=0, max_val=1) > 0):
                dense()

        @block.tensor
        def _(pe):
            pe.wait_ge(consts_dve, 4)
            pe.wait_ge(weights_loaded, 48)
            nc.tensor.transpose(psW[:, 0:P], w_aug[:, 0:D], ident[:, :]).then_inc(wT_ready, 1)
            pe.wait_ge(wT_copied, 1)
            nc.tensor.matmul(psW[:, P:P + 3], wT[:, :], a3[:, :], start=True, stop=True).then_inc(wa_ready, 1)
            pe.wait_ge(w_aug_ready, 1)

            def spread_degrees(q):
                pe.wait_ge(diag_ready, q + 1)
                for i in range(2):
                    mm = nc.tensor.matmul(psR[:, i * 512:(i + 1) * 512], ones[:, :],
                                          diag[:, 4 * i:4 * i + 4, :].rearrange("p o n -> p (o n)"),
                                          start=True, stop=True)
                mm.then_inc(degs_spread, 1)

            def max_tile(q, o):
                t = GT * q + o
                pe.wait_ge(x1_ready, t + 1)
                pe.wait_ge(x1T_copied, t)
                nc.tensor.transpose(psT[:, 0:P], x1w[:, o, :], ident[:, :]).then_inc(x1_turned, 1)
                pe.wait_ge(x1T_copied, t + 1)
                pe.wait_ge(h_saved, t)
                nc.tensor.matmul(psH[:, 0:D + 3], x1T[:, :], w_aug[:, :], start=True, stop=True).then_inc(h_ready, 1)

            spread_degrees(0)
            with pe.Fori(0, GROUPS - 1) as q:
                for o in range(GT):
                    if o == 5:
                        spread_degrees(q + 1)
                    max_tile(q, o)
            for o in range(GT):
                max_tile(GROUPS - 1, o)
            pe.wait_ge(ranked, GROUPS)
            pe.wait_ge(d_diag_ready, 1)
            for c in range(QUARTERS):
                if c >= 2:
                    pe.wait_ge(d_bc_copied, c - 1)
                nc.tensor.matmul(psR[:, (c % 2) * QC:(c % 2 + 1) * QC], ones[:, :], dense_w[1][:, c * QC:(c + 1) * QC],
                                 start=True, stop=True).then_inc(d_spread, 1)

            def turn(q, i, c):
                m = QUARTERS * (PAIRS * q + i) + c
                pe.wait_ge(w_turn_copied, m + 1)
                for k in range(QC // P):
                    at = c * QC + k * P
                    mm = nc.tensor.transpose(psR[:, (c % 2) * QC + k * P:(c % 2) * QC + (k + 1) * P],
                                             dense_w[i % 2][:, at:at + P], ident[:, :])
                mm.then_inc(w_turned, 1)

            def weigh(q, i, c):
                m = QUARTERS * (PAIRS * q + i) + c
                pe.wait_ge(w_turn_copied, m + 3)
                for k in range(QC // P):
                    t = c * (QC // P) + k
                    mm = nc.tensor.matmul(psA[:, 0:D], wTs[:, c % 2, k * P:(k + 1) * P], h_nat[:, t, 0:D],
                                          start=(t == 0), stop=(t == TILES - 1))
                mm.then_inc(w_used, 1)

            pe.wait_ge(d_bc_copied, QUARTERS)
            pe.sem_inc(w_turn_copied, 2)
            pe.sem_inc(w_turned, QUARTERS)
            pe.sem_inc(w_used, 2)
            with pe.Fori(0, GROUPS) as q:
                for i in range(PAIRS):
                    n = PAIRS * q + i
                    pe.wait_ge(dense_weights_ready, n + 1)
                    turn(q, i, 0)
                    pe.wait_ge(neg_ready, n)
                    for c in range(QUARTERS):
                        if c + 1 < QUARTERS:
                            turn(q, i, c + 1)
                        weigh(q, i, c)
            pe.wait_ge(v_checked, 2)
            nc.tensor.matmul(psW[:, 0:GT], ones[:, :], flag_sum[:, :], start=True, stop=True).then_inc(flag_spread, 1)

            def dense():
                with pe.Fori(0, TILES) as t:
                    pe.wait_ge(d_x1_ready, t + 1)
                    nc.tensor.transpose(psT[:, 0:P], x1w[:, 0, :], ident[:, :]).then_inc(d_x1_turned, 1)
                    pe.wait_ge(d_x1T_copied, t + 1)
                    nc.tensor.matmul(psH[:, 0:D + 3], x1T[:, :], w_aug[:, :], start=True, stop=True
                                     ).then_inc(d_h_ready, 1)
                pe.wait_ge(d_rows_loaded, 48)
                with pe.Fori(0, TILES) as t:
                    pe.wait_ge(e_weights_ready, t + 1)
                    for c in range(TILES):
                        pe.wait_ge(e_turn_copied, TILES * t + c)
                        nc.tensor.transpose(psT[:, 0:P], d_p[:, c * P:(c + 1) * P], ident[:, :]
                                            ).then_inc(e_turned, 1)
                        pe.wait_ge(e_turn_copied, TILES * t + c + 1)
                        mm = nc.tensor.matmul(psH[:, 0:D], d_wT[:, c % 2, :], h_rows[:, c, :],
                                              start=(c == 0), stop=(c == TILES - 1))
                    mm.then_inc(e_sum_ready, 1)

            pe.wait_ge(flag_ready, 1)
            with pe.If(pe.value_load(flag_int[0:1, 0:1], min_val=0, max_val=1) > 0):
                dense()

        @block.vector
        def _(dve):
            V = nc.vector
            dve.sem_inc(keyed, 2)
            dve.wait_ge(consts_pool, 7)
            V.tensor_scalar(ident[:, :], ident[:, :], 0.0, None, ALU.is_equal).then_inc(consts_dve, 1)
            V.memset(ones[:, :], 1.0).then_inc(consts_dve, 1)
            V.memset(a3[:, 1:2], 1.0).then_inc(consts_dve, 1)
            V.memset(flag_sum[:, :], 0.0).then_inc(consts_dve, 1)
            for o in range(GT):
                V.memset(slots_of[:, o:o + 1], float(SLOTS[o])).then_inc(consts_dve, 1)
            V.tensor_scalar(rank_base[:, :], rank_base[:, :], (GROWS - 1) / 2, None, ALU.add).then_inc(consts_dve, 1)
            dve.wait_ge(consts_dve, 5 + GT)

            def find(q, o, at, to):
                for s in range(at, to):
                    m = V.max(cand[:, o % 2, 8 * s:8 * s + 8], keys[:, s * SEGMENT:(s + 1) * SEGMENT])
                if to == SEGMENTS:
                    m.then_inc(found, 1)

            def extract(q, o):
                t = GT * q + o
                dve.wait_ge(converted, t + 1)
                dve.wait_ge(found, t)
                V.tensor_tensor(keys.rearrange("p (s c) -> p s c", s=SEGMENTS),
                                adj16[:, o % 2, :].rearrange("p (s c) -> p s c", s=SEGMENTS),
                                local_iota[:, :].unsqueeze(1).to_broadcast([P, SEGMENTS, SEGMENT]),
                                ALU.mult).then_inc(keyed, 1)
                dve.wait_ge(keyed, t + 3)
                dve.sem_inc(dve_passed, 1)
                if o == 0:
                    find(q, o, 0, SEGMENTS)
                else:
                    merge(q, o - 1, lambda k: find(q, o, min(k * 3 // 2, SEGMENTS),
                                                   SEGMENTS if k == EXTRACT_STEPS - 1 else min((k + 1) * 3 // 2, SEGMENTS)))
                if o == GT - 1:
                    merge(q, o)

            def merge(q, o, between=lambda k: None):
                step = Steps(dve, extract_step, EXTRACT_STEPS, GT * q + o)

                def then(instruction):
                    instruction.then_inc(extract_step, 1)
                    between(step.k)
                    step.k += 1
                    dve.wait_ge(extract_step, step.base + step.k)
                    dve.sem_inc(dve_passed, 1)

                c = cand[:, o % 2, :]
                if o == GT - 1:
                    dve.wait_ge(found, GT * q + o + 1)
                then(V.scalar_tensor_tensor(out=gkey[:, 1, :], in0=c, scalar=0.0, in1=seg_base[:, :],
                                            op0=ALU.is_gt, op1=ALU.mult))
                then(V.tensor_tensor(gkey[:, 0, :], gkey[:, 1, :], c, ALU.add))
                for r in range(LIST // 8):
                    eight = listed[:, o, 8 * r:8 * r + 8]
                    then(V.max(eight, gkey[:, r % 2, :]))
                    if r < LIST // 8 - 1:
                        then(V.match_replace(gkey[:, (r + 1) % 2, :], eight, gkey[:, r % 2, :], 0.0))
                step.end()

            def sort(q):
                step = Steps(dve, sort_step, SORT_STEPS, q)
                dve.wait_ge(lists_stored, 16 * GT * q)
                dve.wait_ge(adj_free, GT * (q + 1) + 2)
                degs = rec[:, :, DEG]
                V.tensor_copy(rec[:, :, ROW], row_id[:, bass.ds(q * GT, GT)])
                step(V.tensor_scalar(filled[:, :, :], listed[:, :, :], 0.0, None, ALU.is_gt))
                step(V.tensor_reduce(degs, filled[:, :, :], AX.X, ALU.add))
                V.scalar_tensor_tensor(out=filled[:, :, :], in0=filled[:, :, :], scalar=0.0,
                                       in1=listed[:, :, 0:1].to_broadcast([P, GT, LIST]), op0=ALU.is_equal, op1=ALU.mult)
                V.tensor_tensor(flags[:, 0, :], sums[:, 0, :], degs, ALU.not_equal)
                V.tensor_tensor(flags[:, 1, :], sums[:, 1, :], degs, ALU.not_equal)
                step(V.scalar_tensor_tensor(out=degkey[:, :], in0=degs, scalar=float(GROWS), in1=tie[:, :],
                                            op0=ALU.mult, op1=ALU.add))
                V.tensor_tensor(diag[:, :, :], ident[:, :].unsqueeze(1).to_broadcast([P, GT, P]),
                                degkey[:, :].unsqueeze(2).to_broadcast([P, GT, P]), ALU.mult)
                step(V.tensor_scalar(negkey[:, :], degkey[:, :], -1.0, None, ALU.mult))
                dve.sem_inc(diag_ready, 1)
                step(V.tensor_tensor(filled[:, :, :], filled[:, :, :], listed[:, :, :], ALU.add))
                step(V.tensor_tensor(flag_sum[:, :], flag_sum[:, :], flags[:, 0, :], ALU.add))
                step(V.tensor_tensor(flag_sum[:, :], flag_sum[:, :], flags[:, 1, :], ALU.add))
                step(V.tensor_scalar(rec[:, :, 0:LIST], filled[:, :, :], -1.0, 0.0, ALU.add, ALU.max))
                step.end()

            def check_slots(q):
                step = Steps(dve, check_step, CHECK_STEPS, q)
                dve.wait_ge(sorted_loaded, 16 * (q + 1))
                step(V.tensor_tensor(flags[:, 0, :], srt[:, bass.ds(q * GT, GT), DEG], slots_of[:, :], ALU.is_gt))
                step(V.tensor_tensor(flag_sum[:, :], flag_sum[:, :], flags[:, 0, :], ALU.add))
                step.end()

            def max_tile(q, o):
                t = GT * q + o
                K = SLOTS[o]
                step = Steps(dve, reduce_step, REDUCE_STEPS, t)
                step(V.tensor_scalar(has[:, :], srt[:, q * GT + o, DEG:DEG + 1], 1.0, None, ALU.min))
                dve.wait_ge(own_loaded, 16 * (q + 1))
                dve.wait_ge(gathered[o % 2], 16 * (q * PER_GROUP[o % 2] + UPTO[o]))
                V.tensor_reduce(nmax[:, :], G[:, o % 2, 0:K * D].rearrange("p (k d) -> p d k", d=D),
                                AX.X, ALU.max).then_inc(buffer_free, 1)
                dve.wait_ge(buffer_free, t + 3)
                step(V.scalar_tensor_tensor(out=y0[:, :], in0=nmax[:, :], scalar=has[:, :],
                                            in1=own[:, q * GT + o, :], op0=ALU.mult, op1=ALU.add))
                step(V.bn_stats(stats[:, :], y0[:, :]), dve_passed)
                step(V.bn_aggr(mv[:, :], stats[:, :]))
                V.tensor_scalar(mv[:, 1:2], mv[:, 1:2], EPS, None, ALU.add).then_inc(var_ready, 1)
                step.end()

            def norm_tile(q, o):
                t = GT * q + o
                step = Steps(dve, norm_tile_step, NORM_TILE_STEPS, t)
                dve.wait_ge(std_ready, t + 1)
                step(V.reciprocal(rstd[:, :], std[:, :]))
                dve.wait_ge(x1_turned, GT * q)
                V.tensor_scalar(x1w[:, o, :], y0[:, :], mv[:, 0:1], rstd[:, :], ALU.subtract,
                                ALU.mult).then_inc(x1_ready, 1)
                dve.wait_ge(x1_ready, t + 1)
                dve.sem_inc(dve_passed, 1)
                step(V.tensor_copy(own[:, q * GT + o, :], x1w[:, o, :]))
                step.end()

            def dense_logits(q, i):
                n, b, s_own = PAIRS * q + i, i % 2, hown[:, GT * q + i, D:D + 1]
                link = Steps(dve, shift_step, SHIFT_STEPS, n)
                masked = adj_in[:, b, :].bitcast(F32)
                dve.wait_ge(dense_exp_ready, 2 * n)
                dve.wait_ge(mask_ready, n + 1)
                dve.sem_inc(dve_passed, 1)
                link(V.tensor_tensor_reduce(masked, masked, d_bc[:, :], 1.0, FMIN, ALU.add, ALU.max, mx[:, 1:2]))
                link(V.tensor_scalar(zmax[:, :], mx[:, 1:2], FAR / 50, s_own, ALU.max, ALU.add))
                link(V.scalar_tensor_tensor(out=emax[:, :], in0=zmax[:, :], scalar=ALPHA, in1=zmax[:, :],
                                            op0=ALU.mult, op1=ALU.max))
                V.tensor_tensor(shift[:, 0:1], s_own, emax[:, :], ALU.subtract)
                V.scalar_tensor_tensor(out=shift[:, 1:2], in0=s_own, scalar=ALPHA, in1=emax[:, :],
                                       op0=ALU.mult, op1=ALU.subtract).then_inc(dense_logits_ready, 1)
                link.end()

            def pair(q, i, last):
                n, b, K = PAIRS * q + i, i % 2, SLOTS[PAIRS + i]
                dense, sparse = GT * q + i, GT * q + (PAIRS + i)
                Gt = G[:, b, 0:K * HCOLS].rearrange("p (k c) -> p k c", c=HCOLS)
                step = Steps(dve, pair_step, PAIR_STEPS, n)
                dve.wait_ge(gathered1[b], 16 * (q * PER_GROUP1[b] + UPTO1[i]))
                V.tensor_scalar(pen[:, 0:K], slot_iota[:, 0:K], srt[:, sparse, DEG:DEG + 1], NEG, ALU.is_ge, ALU.mult)
                step(V.tensor_scalar(z[:, 0:K], Gt[:, :, D], hown[:, sparse, D:D + 1], None, ALU.add))
                step(V.scalar_tensor_tensor(out=e[:, 0:K], in0=z[:, 0:K], scalar=ALPHA, in1=z[:, 0:K],
                                            op0=ALU.mult, op1=ALU.max), dve_passed)
                step(V.tensor_tensor_reduce(em[:, 0:K], e[:, 0:K], pen[:, 0:K], 1.0, FMIN, ALU.add, ALU.max,
                                            mx[:, 0:1]))
                V.tensor_scalar(nmx[:, :], mx[:, 0:1], -1.0, None, ALU.mult).then_inc(logits_ready, 1)
                dve.wait_ge(dense_exp_ready, 2 * n + 2)
                dve.sem_inc(dve_passed, 1)
                step(V.scalar_tensor_tensor(out=dense_w[b], in0=dense_w[b], scalar=1.0,
                                            in1=adj_in[:, b, :].bitcast(F32), op0=ALU.mult, op1=ALU.max,
                                            accum_out=zs[:, 1:2]))
                dve.sem_inc(merged, 1)
                step(V.tensor_scalar(zs[:, 1:2], zs[:, 1:2], 0.5, None, ALU.max))
                step(V.tensor_scalar(thz[:, :], zs[:, 1:2], THR, None, ALU.mult))
                V.scalar_tensor_tensor(out=dense_w[b], in0=dense_w[b], scalar=thz[:, :], in1=dense_w[b],
                                       op0=ALU.is_ge, op1=ALU.mult).then_inc(dense_weights_ready, 1)
                step(V.reciprocal(rz[:, 1:2], zs[:, 1:2]))
                step(V.scalar_tensor_tensor(out=gate[:, 1:2], in0=rz[:, 1:2], scalar=THR, in1=srt[:, dense, DEG:DEG + 1],
                                            op0=ALU.is_gt, op1=ALU.mult))
                step(V.tensor_tensor(gate[:, 1:2], gate[:, 1:2], rz[:, 1:2], ALU.mult))
                dve.wait_ge(exp_ready, n + 1)
                link = Steps(dve, sparse_step, SPARSE_STEPS, n)
                link(V.reciprocal(rz[:, 0:1], zs[:, 0:1]))
                V.scalar_tensor_tensor(out=gate[:, 0:1], in0=rz[:, 0:1], scalar=THR, in1=srt[:, sparse, DEG:DEG + 1],
                                       op0=ALU.is_gt, op1=ALU.mult)
                link(V.tensor_scalar(att[:, 0:K], p_exp[:, 0:K], rz[:, 0:1], None, ALU.mult))
                link(V.scalar_tensor_tensor(out=wgt[:, 0:K], in0=att[:, 0:K], scalar=THR, in1=att[:, 0:K],
                                            op0=ALU.is_ge, op1=ALU.mult))
                link(V.tensor_tensor(Gt[:, :, 0:D], Gt[:, :, 0:D],
                                     wgt[:, 0:K].unsqueeze(2).to_broadcast([P, K, D]), ALU.mult))
                V.tensor_reduce(hsum[:, :], Gt[:, :, 0:D].rearrange("p k d -> p d k"), AX.X,
                                ALU.add).then_inc(buffer_free1, 1)
                dve.wait_ge(buffer_free1, n + 3)
                link(V.scalar_tensor_tensor(out=u[:, 0, :], in0=hsum[:, :], scalar=gate[:, 0:1],
                                            in1=hown[:, sparse, 0:D], op0=ALU.mult, op1=ALU.add))
                link.end()
                if not (last and i + 2 >= PAIRS):
                    dense_logits(*((q, i + 2) if i + 2 < PAIRS else (q + 1, i + 2 - PAIRS)))
                dve.wait_ge(w_used, QUARTERS * (n + 1) + 2)
                step(V.scalar_tensor_tensor(out=u[:, 1, :], in0=psA[:, 0:D], scalar=gate[:, 1:2],
                                            in1=hown[:, dense, 0:D], op0=ALU.mult, op1=ALU.add))
                V.tensor_scalar(uneg[:, :, :], u[:, :, :], 0.0, None, ALU.min).then_inc(neg_ready, 1)
                step(V.tensor_scalar(upos[:, :, :], u[:, :, :], 0.0, None, ALU.max))
                dve.wait_ge(uexp_ready, n + 1)
                step(V.scalar_tensor_tensor(out=u[:, :, :], in0=uexp[:, :, :], scalar=-1.0, in1=upos[:, :, :],
                                            op0=ALU.add, op1=ALU.add))
                for j, tile in enumerate((sparse, dense)):
                    o = 2 * i + j
                    dve.wait_ge(out_stored[o], 16 * q)
                    step(V.tensor_tensor(yw[:, o, :], u[:, j, :], own[:, tile, :], ALU.add))
                    step(V.bn_stats(stats[:, :], yw[:, o, :]), dve_passed)
                    step(V.bn_aggr(mvs[:, o, :], stats[:, :]))
                step.end()

            def norm_group(q):
                step = Steps(dve, norm_step, NORM_STEPS, q)
                dve.wait_ge(pair_step, PAIR_STEPS * PAIRS * (q + 1))
                step(V.tensor_scalar(mvs[:, :, 1], mvs[:, :, 1], EPS, None, ALU.add))
                dve.sem_inc(vars_ready, 1)
                dve.wait_ge(stds_ready, q + 1)
                step(V.reciprocal(rstds[:, :], stds[:, :]))
                dve.wait_ge(rid_ready, GT * (q + 1))
                for o in range(GT):
                    V.tensor_scalar(yw[:, o, :], yw[:, o, :], mvs[:, o, 0:1], rstds[:, o:o + 1], ALU.subtract,
                                    ALU.mult).then_inc(out_ready, 1)
                step.end()

            for o in range(GT):
                extract(0, o)
            sort(0)
            with dve.Fori(0, GROUPS - 1) as q:
                check_slots(q)
                for o in range(GT):
                    for i in range(EXTRACTS[o]):
                        extract(q + 1, FIRST[o] + i)
                    if o:
                        norm_tile(q, o - 1)
                    max_tile(q, o)
                    if o == 5:
                        sort(q + 1)
                norm_tile(q, GT - 1)
            check_slots(GROUPS - 1)
            for o in range(GT):
                max_tile(GROUPS - 1, o)
                norm_tile(GROUPS - 1, o)
            dve.wait_ge(hrow_ready, TILES)
            V.tensor_reduce(least[:, :], v_own[:, :], AX.X, ALU.min).then_inc(v_checked, 1)
            dve.wait_ge(adj_free, TILES + 2)
            dve.wait_ge(h_nat_loaded, 16)
            V.tensor_tensor(dense_w[1].rearrange("p (t n) -> p t n", n=P),
                            ident[:, :].unsqueeze(1).to_broadcast([P, TILES, P]),
                            h_nat[:, :, D].unsqueeze(2).to_broadcast([P, TILES, P]), ALU.mult).then_inc(d_diag_ready, 1)
            dve.wait_ge(v_checked, 1)
            V.scalar_tensor_tensor(out=flag_sum[:, 0:1], in0=least[:, :], scalar=0.0, in1=flag_sum[:, 0:1],
                                   op0=ALU.is_equal, op1=ALU.add).then_inc(v_checked, 1)
            dense_logits(0, 0)
            dense_logits(0, 1)
            with dve.Fori(0, GROUPS - 1) as q:
                for i in range(PAIRS):
                    pair(q, i, False)
                norm_group(q)
            for i in range(PAIRS):
                pair(GROUPS - 1, i, True)
            norm_group(GROUPS - 1)
            dve.wait_ge(flag_spread, 1)
            V.reduce_max(flag[:, :], psW[:, 0:GT], axis=AX.X).then_inc(flag_checked, 1)
            dve.wait_ge(flag_checked, 1)
            V.tensor_scalar(flag_int[:, :], flag[:, :], 1.0, None, ALU.min).then_inc(flag_ready, 1)

            def dense_max(t):
                step = Steps(dve, d_max_step, DENSE_MAX_STEPS, t)
                dve.wait_ge(d_tile_loaded, 32 * (t + 1))
                V.tensor_scalar(d_bias, d_adj, 0.0, FMIN, ALU.is_equal, ALU.mult)
                V.memset(d_acc[:, :], FMIN)
                step(V.tensor_scalar(d_sum, d_adj, 0.0, 0.0, ALU.not_equal, ALU.add, accum_out=cnt[:, :]))
                step(V.tensor_scalar(d_has[:, :], cnt[:, :], 1.0, None, ALU.min), dve_passed)
                with dve.Fori(0, CHUNKS // 2) as c:
                    for b in range(2):
                        chunk = t * CHUNKS + c * 2 + b
                        link = Steps(dve, d_chunk_step, CHUNK_STEPS, chunk)
                        dve.wait_ge(d_chunk_loaded[b], 16 * (t * (CHUNKS // 2) + c + 1))
                        summed = d_sum.rearrange("p (j d) -> p j d", d=D)
                        V.tensor_tensor(summed, G[:, b, 0:CHUNK * D].rearrange("p (j d) -> p j d", d=D),
                                        d_bias[:, bass.ds((c * 2 + b) * CHUNK, CHUNK)].unsqueeze(2)
                                        .to_broadcast([P, CHUNK, D]), ALU.add).then_inc(d_chunk_used, 1)
                        dve.wait_ge(d_chunk_used, chunk + 3)
                        link(V.tensor_reduce(d_max[:, :], d_sum.rearrange("p (j d) -> p d j", d=D), AX.X, ALU.max))
                        link(V.tensor_tensor(d_acc[:, :], d_acc[:, :], d_max[:, :], ALU.max))
                        link.end()
                step(V.scalar_tensor_tensor(out=y0[:, :], in0=d_acc[:, :], scalar=d_has[:, :], in1=d_x[:, :],
                                            op0=ALU.mult, op1=ALU.add))
                step(V.bn_stats(stats[:, :], y0[:, :]), dve_passed)
                step(V.bn_aggr(mv[:, :], stats[:, :]))
                V.tensor_scalar(mv[:, 1:2], mv[:, 1:2], EPS, None, ALU.add).then_inc(d_var_ready, 1)
                dve.wait_ge(d_std_ready, t + 1)
                step(V.reciprocal(rstd[:, :], std[:, :]))
                V.tensor_scalar(x1w[:, 0, :], y0[:, :], mv[:, 0:1], rstd[:, :], ALU.subtract,
                                ALU.mult).then_inc(d_x1_ready, 1)
                step.end()

            def dense_attend(t):
                step = Steps(dve, e_step, DENSE_ATTEND_STEPS, t)
                dve.wait_ge(e_tile_loaded, 48 * (t + 1))
                step(V.scalar_tensor_tensor(out=d_vm, in0=d_adj, scalar=0.0, in1=v_rows, op0=ALU.is_gt, op1=ALU.mult))
                step(V.reduce_sum(cnt[:, :], d_vm, axis=AX.X))
                step(V.tensor_scalar(d_p, d_rows, s_all[:, bass.ds(t, 1)], None, ALU.add))
                step(V.scalar_tensor_tensor(out=d_z, in0=d_p, scalar=ALPHA, in1=d_p, op0=ALU.mult, op1=ALU.max))
                step(V.tensor_tensor(d_z, d_z, d_vm, ALU.mult))
                step(V.tensor_scalar(d_p, d_vm, 1.0, -NEG, ALU.subtract, ALU.mult))
                step(V.tensor_tensor(d_z, d_z, d_p, ALU.add))
                step(V.reduce_max(mx[:, 0:1], d_z, axis=AX.X))
                V.tensor_scalar(nmx[:, :], mx[:, 0:1], -1.0, None, ALU.mult).then_inc(e_logits_ready, 1)
                dve.wait_ge(e_exp_ready, t + 1)
                step(V.reciprocal(rz[:, 0:1], zs[:, 0:1]))
                step(V.scalar_tensor_tensor(out=d_z, in0=d_p, scalar=rz[:, 0:1], in1=d_vm, op0=ALU.mult, op1=ALU.mult))
                step(V.reduce_max(topa[:, :], d_z, axis=AX.X))
                step(V.scalar_tensor_tensor(out=gate[:, 0:1], in0=topa[:, :], scalar=THR, in1=cnt[:, :],
                                            op0=ALU.is_gt, op1=ALU.mult))
                V.scalar_tensor_tensor(out=d_p, in0=d_z, scalar=THR, in1=d_z, op0=ALU.is_ge,
                                       op1=ALU.mult).then_inc(e_weights_ready, 1)
                dve.wait_ge(e_sum_ready, t + 1)
                step(V.tensor_scalar(hsum[:, :], psH[:, 0:D], gate[:, 0:1], None, ALU.mult))
                step(V.tensor_tensor(u[:, 0, :], hsum[:, :], h_own[:, :], ALU.add))
                V.tensor_scalar(uneg[:, 0, :], u[:, 0, :], 0.0, None, ALU.min).then_inc(e_neg_ready, 1)
                step(V.tensor_scalar(upos[:, 0, :], u[:, 0, :], 0.0, None, ALU.max))
                dve.wait_ge(e_uexp_ready, t + 1)
                step(V.scalar_tensor_tensor(out=u[:, 0, :], in0=uexp[:, 0, :], scalar=-1.0, in1=upos[:, 0, :],
                                            op0=ALU.add, op1=ALU.add))
                step(V.tensor_tensor(y0[:, :], u[:, 0, :], d_x[:, :], ALU.add))
                step(V.bn_stats(stats[:, :], y0[:, :]), dve_passed)
                step(V.bn_aggr(mv[:, :], stats[:, :]))
                V.tensor_scalar(mv[:, 1:2], mv[:, 1:2], EPS, None, ALU.add).then_inc(e_var_ready, 1)
                dve.wait_ge(e_std_ready, t + 1)
                step(V.reciprocal(rstd[:, :], std[:, :]))
                V.tensor_scalar(yw[:, 0, :], y0[:, :], mv[:, 0:1], rstd[:, :], ALU.subtract,
                                ALU.mult).then_inc(e_y_ready, 1)
                step.end()

            def dense():
                dve.sem_inc(d_chunk_used, 2)
                for o in range(GT):
                    dve.wait_ge(out_stored[o], 16 * GROUPS)
                with dve.Fori(0, TILES) as t:
                    dense_max(t)
                dve.wait_ge(d_rows_loaded, 48)
                with dve.Fori(0, TILES) as t:
                    dense_attend(t)

            dve.wait_ge(flag_ready, 1)
            with dve.If(dve.value_load(flag_int[0:1, 0:1], min_val=0, max_val=1) > 0):
                dense()


_INS = ['x', 'adj', 'L1_gnn_W', 'L1_gnn_a']


def kernel(**inputs):
    import numpy as _np
    import concourse.bacc as _bacc
    from concourse import mybir as _mybir
    from concourse.bass_utils import run_bass_kernel_spmd as _run

    nc = _bacc.Bacc("TRN2", target_bir_lowering=False, num_devices=1)
    arrays, args = {}, []
    for name in _INS:
        a = _np.ascontiguousarray(inputs[name])
        arrays[f"in_{name}_dram"] = a
        args.append(nc.dram_tensor(f"in_{name}_dram", a.shape, _mybir.dt.from_np(a.dtype), kind="ExternalInput").ap())
    args.append(nc.dram_tensor("out_0_dram", (N, D), _mybir.dt.float32, kind="ExternalOutput").ap())
    args.append(nc.dram_tensor("lists_dram", (N, REC), _mybir.dt.float32, kind="Internal").ap())
    args.append(nc.dram_tensor("htab_dram", (N, HCOLS), _mybir.dt.float32, kind="Internal").ap())
    for name, cols in ("x1_dram", D), ("h_dram", D), ("d_dram", 1), ("v_dram", 1):
        args.append(nc.dram_tensor(name, (N, cols), _mybir.dt.float32, kind="Internal").ap())
    build(nc, *args)
    r = _run(nc, [arrays], core_ids=[0])
    return r.results[0]["out_0_dram"]
```

```python
from contextlib import ExitStack

import concourse.bass as bass
import concourse.mybir as mybir

ALU = mybir.AluOpType
ACT = mybir.ActivationFunctionType
AX = mybir.AxisListType
F32, BF16, I32, U32 = mybir.dt.float32, mybir.dt.bfloat16, mybir.dt.int32, mybir.dt.uint32

P = 128
N = 4096
D = 128
TILES = N // P
GT = 8
GROUPS = TILES // GT
GROWS = GT * P
SEGMENT = 256
SEGMENTS = N // SEGMENT
CAND = 8 * SEGMENTS
LIST = 40
DEG, ROW, XCOL = LIST, LIST + 1, LIST + 2
REC = XCOL + D
TOP, DIRECT, MORE = 32, 25, 3
BANDS = P // TOP
SLOTS = [DIRECT + MORE, 21, 19, 18, 17, 15, 14, 12]
HCOLS = D + 1
CHUNK = 32
CHUNKS = N // CHUNK
GBUF = max(*SLOTS, CHUNK) * D
SCOLS = max(SLOTS[GT // 2:]) * HCOLS
PAIRS = GT // 2
BANK = 512
PIECES = 4
PIECE = N // PIECES
EXTRACTS = [3, 1, 2, 1, 1, 0, 0, 0]
SORT_AT = 4
PLACE_AT = 6
FIRST = [sum(EXTRACTS[:o]) for o in range(GT)]
CONVERTED = [min(FIRST[o] + EXTRACTS[o] + 2, GT) for o in range(GT)]
STORED = [[], [0, 1, 2], [3, 4, 5], [6, 7]]
PERMUTED = [[2, 3], [4, 5], [6, 7], [], [], [], [], []]
EPS, THR, ALPHA, NEG = 1e-5, 1e-4, 0.2, -1e9
FAR = NEG / ALPHA
FMIN = -3.4028234663852886e38

UPTO = [sum(SLOTS[i] for i in range(o % 2, o + 1, 2)) for o in range(GT)]
PER_GROUP = [UPTO[GT - 2], UPTO[GT - 1]]
UPTO1 = [sum(SLOTS[PAIRS + j] for j in range(i % 2, i + 1, 2)) for i in range(PAIRS)]
PER_GROUP1 = [UPTO1[PAIRS - 2], UPTO1[PAIRS - 1]]

EXTRACT_STEPS = 11
SORT_STEPS = 8
CHECK_STEPS = 2
REDUCE_STEPS = 4
TOP_STEPS = 3
NORM_TILE_STEPS = 2
CHUNK_STEPS = 2
DENSE_MAX_STEPS = 6
DENSE_ATTEND_STEPS = 20
SPARSE_LOGITS_STEPS = 3
SPARSE_STEPS = 2
SHIFT_STEPS = 3
WEIGH_STEPS = 3
GATE_STEPS = 3
FINISH_STEPS = 6
NORM_STEPS = 1


class Steps:

    def __init__(self, eng, sem, per, turn):
        self.eng, self.sem, self.per, self.base, self.k = eng, sem, per, turn * per, 0

    def __call__(self, instruction, passed=None):
        self.k += 1
        instruction.then_inc(self.sem, 1)
        self.eng.wait_ge(self.sem, self.base + self.k)
        if passed is not None:
            self.eng.sem_inc(passed, 1)

    def end(self):
        assert self.k == self.per, (self.k, self.per)


def build(nc, x, adj, W, a, out, htab, x1_all, h_all, d_all, v_all):
    with ExitStack() as ctx:
        def sb(name, shape, dt=F32):
            return ctx.enter_context(nc.sbuf_tensor(name, shape, dt))

        def ps(name, shape):
            return ctx.enter_context(nc.psum_tensor(name, shape, F32))

        def sem(name):
            return ctx.enter_context(nc.semaphore(name))

        ident = sb("ident", [P, P])
        ones = sb("ones", [P, P])
        local_iota = sb("local_iota", [P, SEGMENT], BF16)
        seg_base = sb("seg_base", [P, CAND])
        row_id = sb("row_id", [P, TILES])
        tie = sb("tie", [P, GT])
        tile_base = sb("tile_base", [P, GT])
        slot_iota = sb("slot_iota", [P, LIST])
        slots_of = sb("slots_of", [P, GT])
        w_aug = sb("w_aug", [P, D + 3])
        wT = sb("wT", [P, D])
        a3 = sb("a3", [P, 3])
        adj_in = sb("adj_in", [P, 2, N], I32)
        adj16 = sb("adj16", [P, 2, N], BF16)
        scratch16 = sb("scratch16", [P, 2, N], BF16)
        squares, keys = scratch16[:, 0, :], scratch16[:, 1, :]
        sums = sb("sums", [P, 2, GT])
        cand = sb("cand", [P, 2, CAND])
        gkey = sb("gkey", [P, 2, CAND])
        listed = sb("listed", [P, GT, LIST])
        filled = sb("filled", [P, GT, LIST])
        flags = sb("flags", [P, 2, GT])
        flag_sum = sb("flag_sum", [P, GT])
        rec = sb("rec", [P, GT, REC])
        degkey = sb("degkey", [P, GT])
        diag = sb("diag", [P, GT, P])
        negkey = sb("negkey", [P, GT])
        beaten = sb("beaten", [P, GROWS], BF16)
        rank = sb("rank", [P, GT])
        place = sb("place", [P, GT, GT])
        srt = sb("srt", [P, TILES, XCOL])
        own = sb("own", [P, TILES, D])
        idx = sb("idx", [P, GT, LIST], U32)
        more = sb("more", [P, MORE], U32)
        bands = sb("bands", [P, BANDS + 1, D])
        rid = sb("rid", [P, GT], U32)
        G = sb("G", [P, 2, GBUF])
        nmax = sb("nmax", [P, D])
        has = sb("has", [P, 1])
        y0 = sb("y0", [P, D])
        stats = sb("stats", [P, 2, 6])
        mv = sb("mv", [P, 2])
        std = sb("std", [P, 1])
        rstd = sb("rstd", [P, 1])
        x1w = sb("x1w", [P, GT, D])
        x1T = sb("x1T", [P, P])
        hown = sb("hown", [P, TILES, D + 1])
        hrow = sb("hrow", [P, GT, HCOLS])
        v_own = sb("v_own", [P, TILES])
        sgn = sb("sgn", [P, 1])
        z = sb("z", [P, LIST])
        e = sb("e", [P, LIST])
        pen = sb("pen", [P, LIST])
        em = sb("em", [P, LIST])
        mx = sb("mx", [P, 2])
        nmx = sb("nmx", [P, 1])
        zmax = sb("zmax", [P, 1])
        emax = sb("emax", [P, 1])
        shift = sb("shift", [P, 2])
        p_exp = sb("p_exp", [P, LIST])
        zs = sb("zs", [P, 2])
        rz = sb("rz", [P, 2])
        thz = sb("thz", [P, 1])
        gate = sb("gate", [P, 3])
        least = sb("least", [P, 1])
        att = sb("att", [P, LIST])
        wgt = sb("wgt", [P, LIST])
        hsum = sb("hsum", [P, D])
        u = sb("u", [P, 2, D])
        upos = sb("upos", [P, 2, D])
        uneg = sb("uneg", [P, 2, D])
        uexp = sb("uexp", [P, 2, D])
        adj_rid = sb("adj_rid", [P, PAIRS], U32)
        h_nat = sb("h_nat", [P, TILES, HCOLS])
        d_bc = sb("d_bc", [P, N])
        wTs = [diag[:, :, :].rearrange("p o n -> p (o n)"), rec[:, :, :].rearrange("p o r -> p (o r)")[:, 0:PIECE]]
        select = [diag, d_bc[:, 0:GROWS].rearrange("p (o n) -> p o n", n=P)]
        G_flat = G[:, :, :].rearrange("p b n -> p (b n)")
        gathered_h = [G_flat[:, b * SCOLS:(b + 1) * SCOLS].rearrange("p (k c) -> p k c", c=HCOLS) for b in range(2)]
        assert 2 * SCOLS + max(SLOTS[PAIRS:]) * P <= 2 * GBUF
        weight_diag = G_flat[:, 2 * SCOLS:2 * SCOLS + max(SLOTS[PAIRS:]) * P].rearrange("p (k n) -> p k n", n=P)
        dense_w = [adj16[:, :, :].rearrange("p b n -> p (b n)").bitcast(F32),
                   scratch16[:, :, :].rearrange("p b n -> p (b n)").bitcast(F32)]
        yw, normed = x1w, hrow
        mvs = sb("mvs", [P, GT, 2])
        stds = sb("stds", [P, GT])
        rstds = sb("rstds", [P, GT])

        flag = sb("flag", [P, 1])
        flag_int = sb("flag_int", [P, 1], I32)
        s_all = sb("s_all", [P, TILES])
        topa = sb("topa", [P, 1])
        cnt = sb("cnt", [P, 1])
        d_has = sb("d_has", [P, 1])
        d_acc, d_max, d_x, h_own = (rows[:, 1, :] for rows in (u, upos, uneg, uexp))
        d_h = sb("d_h", [P, D + 3])
        d_wT = [piece[:, 0:P] for piece in wTs]
        d_adj = adj_in[:, 0, :]
        d_bias, d_sum = d_bc[:, :], own[:, :, :].rearrange("p t d -> p (t d)")
        d_z, d_vm = dense_w[0], d_sum
        d_p = adj_in[:, 1, :].bitcast(F32)
        d_rows, v_rows = d_bc[:, :], dense_w[1]
        h_rows = G[:, 0, 0:N].rearrange("p (t d) -> p t d", d=D)

        psR = ps("psR", [P, GROWS])
        psT = ps("psT", [P, BANK])
        psH = ps("psH", [P, BANK])
        psV = ps("psV", [P, GROWS])
        psW = psV[:, 0:BANK]
        psP = [psR, psV]
        psA = ps("psA", [P, 2, BANK])
        psS = [psT, psH]

        consts_pool = sem("consts_pool")
        consts_dve = sem("consts_dve")
        weights_loaded = sem("weights_loaded")
        wT_ready = sem("wT_ready")
        wT_copied = sem("wT_copied")
        wa_ready = sem("wa_ready")
        w_aug_ready = sem("w_aug_ready")
        adj_loaded = [sem(f"adj_loaded{b}") for b in range(2)]
        x_loaded = sem("x_loaded")
        adj_free = sem("adj_free")
        converted = sem("converted")
        keyed = sem("keyed")
        found = sem("found")
        extract_step = sem("extract_step")
        sort_step = sem("sort_step")
        rank_step = sem("rank_step")
        check_step = sem("check_step")
        diag_ready = sem("diag_ready")
        degs_spread = sem("degs_spread")
        place_step = sem("place_step")
        select_ready = sem("select_ready")
        permuted = sem("permuted")
        sorted_copied = sem("sorted_copied")
        gathered = [sem(f"gathered{b}") for b in range(2)]
        buffer_free = sem("buffer_free")
        reduce_step = sem("reduce_step")
        top_step = sem("top_step")
        var_ready = sem("var_ready")
        norm_tile_step = sem("norm_tile_step")
        std_ready = sem("std_ready")
        x1_ready = sem("x1_ready")
        x1_turned = sem("x1_turned")
        x1T_copied = sem("x1T_copied")
        h_ready = sem("h_ready")
        h_saved = sem("h_saved")
        hrow_ready = sem("hrow_ready")
        act_step = sem("act_step")
        row_stored = [sem(f"row_stored{o}") for o in range(GT)]
        v_checked = sem("v_checked")
        idx1_ready = sem("idx1_ready")
        gathered1 = [sem(f"gathered1_{b}") for b in range(2)]
        buffer_free1 = sem("buffer_free1")
        adj_rid_ready = sem("adj_rid_ready")
        rows_gathered = [sem(f"rows_gathered{b}") for b in range(2)]
        h_nat_loaded = [sem(f"h_nat_loaded{q}") for q in range(GROUPS)]
        d_diag_ready = sem("d_diag_ready")
        d_spread = sem("d_spread")
        d_bc_copied = sem("d_bc_copied")
        mask_ready = sem("mask_ready")
        shift_step = sem("shift_step")
        dense_logits_ready = sem("dense_logits_ready")
        dense_exp_ready = sem("dense_exp_ready")
        merged = sem("merged")
        dense_weights_ready = sem("dense_weights_ready")
        w_turned = sem("w_turned")
        w_turn_copied = sem("w_turn_copied")
        w_used = sem("w_used")
        sparse_step = sem("sparse_step")
        sparse_logits_step = sem("sparse_logits_step")
        weigh_step = sem("weigh_step")
        gate_step = sem("gate_step")
        finish_step = sem("finish_step")
        logits_ready = sem("logits_ready")
        exp_ready = sem("exp_ready")
        sparse_weights_ready = sem("sparse_weights_ready")
        weight_diag_ready = sem("weight_diag_ready")
        neg_ready = sem("neg_ready")
        uexp_ready = sem("uexp_ready")
        vars_ready = sem("vars_ready")
        stds_ready = sem("stds_ready")
        norm_step = sem("norm_step")
        rid1_ready = sem("rid1_ready")
        out_ready = sem("out_ready")
        flag_spread = sem("flag_spread")
        flag_checked = sem("flag_checked")
        flag_ready = sem("flag_ready")
        d_tile_loaded = sem("d_tile_loaded")
        d_chunk_loaded = [sem(f"d_chunk_loaded{b}") for b in range(2)]
        d_chunk_used = sem("d_chunk_used")
        d_chunk_step = sem("d_chunk_step")
        d_max_step = sem("d_max_step")
        d_var_ready = sem("d_var_ready")
        d_std_ready = sem("d_std_ready")
        d_x1_ready = sem("d_x1_ready")
        d_x1_turned = sem("d_x1_turned")
        d_x1T_copied = sem("d_x1T_copied")
        d_h_ready = sem("d_h_ready")
        d_h_saved = sem("d_h_saved")
        d_tile_stored = sem("d_tile_stored")
        d_rows_loaded = sem("d_rows_loaded")
        e_tile_loaded = sem("e_tile_loaded")
        e_step = sem("e_step")
        e_logits_ready = sem("e_logits_ready")
        e_exp_ready = sem("e_exp_ready")
        e_weights_ready = sem("e_weights_ready")
        e_turned = sem("e_turned")
        e_turn_copied = sem("e_turn_copied")
        e_sum_ready = sem("e_sum_ready")
        e_neg_ready = sem("e_neg_ready")
        e_uexp_ready = sem("e_uexp_ready")
        e_var_ready = sem("e_var_ready")
        e_std_ready = sem("e_std_ready")
        e_y_ready = sem("e_y_ready")
        e_out_stored = sem("e_out_stored")
        pool_passed = sem("pool_passed")
        sp_passed = sem("sp_passed")
        dve_passed = sem("dve_passed")
        act_passed = sem("act_passed")

        adj_t = adj.rearrange("(t p) n -> t p n", p=P)
        x_t = x.rearrange("(t p) d -> t p d", p=P)
        x_c = x.rearrange("(c j) d -> c (j d)", j=CHUNK)
        x1_t = x1_all.rearrange("(t p) d -> t p d", p=P)
        h_t = h_all.rearrange("(t p) d -> t p d", p=P)
        d_t = d_all.rearrange("(t p) c -> t p c", p=P)
        v_t = v_all.rearrange("(t p) c -> t p c", p=P)
        out_t = out.rearrange("(t p) d -> t p d", p=P)
        x_g = x.rearrange("(q o p) d -> q p o d", o=GT, p=P)
        htab_g = htab.rearrange("(q o p) c -> q p o c", o=GT, p=P)

        def by_pair(tiles):
            return tiles.rearrange("p (m i) c -> p i m c", i=PAIRS)

        block = ctx.enter_context(nc.Block())

        @block.sync
        def _(sp):
            sp.dma_start(w_aug[:, 0:D], W).then_inc(weights_loaded, 16)
            with nc.allow_non_contiguous_dma("two columns of 128"):
                sp.dma_start(a3[:, 0:1], a[D:2 * D, :]).then_inc(weights_loaded, 16)
                sp.dma_start(a3[:, 2:3], a[0:D, :]).then_inc(weights_loaded, 16)

            with sp.Fori(0, GROUPS) as q:
                for o in range(GT):
                    sp.wait_ge(adj_free, GT * q + o + 1)
                    sp.dma_start(adj_in[:, o % 2, :], adj_t[q * GT + o]).then_inc(adj_loaded[o % 2], 16)
                sp.wait_ge(permuted, GT * q + 2)
                sp.dma_start(rec[:, :, XCOL:REC], x_g[q]).then_inc(x_loaded, 16)
            for q in range(GROUPS):
                for o in range(GT):
                    sp.wait_ge(row_stored[o], 16 * (q + 1))
                sp.dma_start(h_nat[:, q * GT:(q + 1) * GT, :], htab_g[q]).then_inc(h_nat_loaded[q], 16)

            def dense():
                for o in range(GT):
                    sp.wait_ge(row_stored[o], 16 * 2 * GROUPS)
                with sp.Fori(0, TILES) as t:
                    sp.dma_start(d_adj, adj_t[t]).then_inc(d_tile_loaded, 16)
                    sp.dma_start(d_x[:, :], x_t[t]).then_inc(d_tile_loaded, 16)
                    with sp.Fori(0, CHUNKS // 2) as c:
                        for b in range(2):
                            sp.wait_ge(d_chunk_used, t * CHUNKS + c * 2 + b + 1)
                            sp.dma_start(G[:, b, 0:CHUNK * D], x_c[c * 2 + b].partition_broadcast(P)
                                         ).then_inc(d_chunk_loaded[b], 16)
                    sp.wait_ge(d_h_saved, t + 1)
                    sp.dma_start(x1_t[t], x1w[:, 0, :]).then_inc(d_tile_stored, 16)
                    sp.dma_start(h_t[t], d_h[:, 0:D]).then_inc(d_tile_stored, 16)
                    with nc.allow_non_contiguous_dma("a column of 128"):
                        sp.dma_start(d_t[t], d_h[:, D:D + 1]).then_inc(d_tile_stored, 16)
                        sp.dma_start(v_t[t], d_h[:, D + 1:D + 2]).then_inc(d_tile_stored, 16)
                    sp.wait_ge(d_tile_stored, 64 * (t + 1))
                    sp.sem_inc(sp_passed, 1)
                sp.dma_start(d_rows, d_all.rearrange("n c -> (n c)").partition_broadcast(P)).then_inc(d_rows_loaded, 16)
                sp.dma_start(v_rows, v_all.rearrange("n c -> (n c)").partition_broadcast(P)).then_inc(d_rows_loaded, 16)
                sp.dma_start(h_rows, h_all.rearrange("(t p) d -> p t d", p=P)).then_inc(d_rows_loaded, 16)
                with sp.Fori(0, TILES) as t:
                    sp.dma_start(d_adj, adj_t[t]).then_inc(e_tile_loaded, 16)
                    sp.dma_start(d_x[:, :], x1_t[t]).then_inc(e_tile_loaded, 16)
                    sp.dma_start(h_own[:, :], h_t[t]).then_inc(e_tile_loaded, 16)
                    sp.wait_ge(e_y_ready, t + 1)
                    sp.dma_start(out_t[t], yw[:, 0, :]).then_inc(e_out_stored, 16)
                    sp.wait_ge(e_out_stored, 16 * (t + 1))
                    sp.sem_inc(sp_passed, 1)

            sp.wait_ge(flag_ready, 1)
            with sp.If(sp.value_load(flag_int[0:1, 0:1], min_val=0, max_val=1) > 0):
                dense()

        @block.gpsimd
        def _(pool):
            pool.sem_inc(buffer_free, 2)
            pool.sem_inc(buffer_free1, 2)
            pool.iota(ident[:, :], [[-1, P]], base=0, channel_multiplier=1,
                      allow_small_or_imprecise_dtypes=True).then_inc(consts_pool, 1)
            pool.iota(local_iota[:, :], [[1, SEGMENT]], base=1, channel_multiplier=0,
                      allow_small_or_imprecise_dtypes=True).then_inc(consts_pool, 1)
            pool.iota(seg_base[:, :], [[SEGMENT, SEGMENTS], [0, 8]], base=0, channel_multiplier=0,
                      allow_small_or_imprecise_dtypes=True).then_inc(consts_pool, 1)
            pool.iota(row_id[:, :], [[P, TILES]], base=0, channel_multiplier=1,
                      allow_small_or_imprecise_dtypes=True).then_inc(consts_pool, 1)
            pool.iota(tie[:, :], [[P, GT]], base=0, channel_multiplier=1,
                      allow_small_or_imprecise_dtypes=True).then_inc(consts_pool, 1)
            pool.iota(tile_base[:, :], [[-P, GT]], base=0, channel_multiplier=0,
                      allow_small_or_imprecise_dtypes=True).then_inc(consts_pool, 1)
            pool.iota(slot_iota[:, :], [[1, LIST]], base=0, channel_multiplier=0,
                      allow_small_or_imprecise_dtypes=True).then_inc(consts_pool, 1)

            def gathers(turn, o, table, width):
                pool.wait_ge(sorted_copied, GT * turn + o + 3)
                pool.wait_ge(buffer_free, GT * turn + o + 1)
                pool.sem_inc(pool_passed, 1)
                for k in range(SLOTS[o]):
                    direct = o or k < DIRECT
                    pool.indirect_dma_start(
                        out=G[:, o % 2, k * width:(k + 1) * width], out_offset=None, in_=table,
                        in_offset=bass.IndirectOffsetOnAxis(
                            ap=idx[:, o, k:k + 1] if direct else more[:, k - DIRECT:k - DIRECT + 1], axis=0),
                    ).then_inc(gathered[o % 2], 16)

            def store_hrow(q, o):
                pool.wait_ge(hrow_ready, GT * q + o + 1)
                pool.sem_inc(pool_passed, 1)
                pool.indirect_dma_start(
                    out=htab, out_offset=bass.IndirectOffsetOnAxis(ap=rid[:, o:o + 1], axis=0),
                    in_=hrow[:, o, :], in_offset=None).then_inc(row_stored[o], 16)

            def store_out(q, o):
                pool.wait_ge(rid1_ready, q + 1)
                pool.wait_ge(out_ready, GT * q + o + 1)
                pool.sem_inc(pool_passed, 1)
                pool.indirect_dma_start(
                    out=out, out_offset=bass.IndirectOffsetOnAxis(ap=rid[:, o:o + 1], axis=0),
                    in_=normed[:, o, 0:D], in_offset=None).then_inc(row_stored[o], 16)

            def gather_adj(q, i, merged_before=True):
                n = PAIRS * q + i
                pool.wait_ge(adj_rid_ready, n + 1)
                if merged_before:
                    pool.wait_ge(merged, n - 1)
                else:
                    pool.wait_ge(adj_free, TILES + 2)
                pool.sem_inc(pool_passed, 1)
                pool.indirect_dma_start(
                    out=adj_in[:, i % 2, :], out_offset=None, in_=adj,
                    in_offset=bass.IndirectOffsetOnAxis(ap=adj_rid[:, i:i + 1], axis=0),
                ).then_inc(rows_gathered[i % 2], 16)

            def max_group(q, first=False, last=False):
                for o in range(GT):
                    gathers(q, o, x, D)
                    if last:
                        for i in range(2 * o, min(2 * o + 2, GT)):
                            store_hrow(q - 1, i)
                        if o >= 2:
                            store_hrow(q, o - 2)
                        if o in (4, 5):
                            gather_adj(0, o - 4, merged_before=False)
                    elif not first:
                        store_hrow(q - 1, o)

            max_group(0, first=True)
            with pool.Fori(1, GROUPS - 1) as q:
                max_group(q)
            max_group(GROUPS - 1, last=True)
            for o in (GT - 2, GT - 1):
                store_hrow(GROUPS - 1, o)

            def gather_h(q, i, between=None):
                n = PAIRS * q + i
                pool.wait_ge(idx1_ready, n + 1)
                pool.wait_ge(buffer_free1, n + 1)
                pool.sem_inc(pool_passed, 1)
                K = SLOTS[PAIRS + i]
                for k in range(K):
                    if between and k == K // 2:
                        between()
                    pool.indirect_dma_start(
                        out=gathered_h[i % 2][:, k, :], out_offset=None, in_=htab,
                        in_offset=bass.IndirectOffsetOnAxis(ap=idx[:, PAIRS + i, k:k + 1], axis=0),
                    ).then_inc(gathered1[i % 2], 16)

            def pair(q, i, last=False, stores=True):
                q1, i1 = (q, i + 1) if i + 1 < PAIRS else (q + 1, 0)
                q2, i2 = (q, i + 2) if i + 2 < PAIRS else (q + 1, i + 2 - PAIRS)
                if not (last and i + 1 == PAIRS):
                    gather_h(q1, i1, (lambda: gather_adj(q2, i2)) if not (last and i + 2 >= PAIRS) else None)
                if i and stores:
                    for o in STORED[i]:
                        store_out(q - 1, o)

            for o in range(GT):
                pool.wait_ge(row_stored[o], 16 * GROUPS)
            gather_h(0, 0)
            for i in range(PAIRS):
                pair(0, i, stores=False)
            with pool.Fori(1, GROUPS - 1) as q:
                for i in range(PAIRS):
                    pair(q, i)
            for i in range(PAIRS):
                pair(GROUPS - 1, i, last=True)
            for o in range(GT):
                store_out(GROUPS - 1, o)
            for o in range(GT):
                pool.wait_ge(row_stored[o], 16 * 2 * GROUPS)

        @block.scalar
        def _(act):
            act.sem_inc(adj_free, 2)

            def convert(q, o):
                t = GT * q + o
                if o == 0:
                    act.wait_ge(sort_step, SORT_STEPS * q)
                act.wait_ge(adj_loaded[o % 2], 16 * (GT // 2 * q + o // 2 + 1))
                act.wait_ge(adj_free, t + 2)
                act.wait_ge(keyed, t + 1)
                nc.scalar.activation(adj16[:, o % 2, :], adj_in[:, o % 2, :], ACT.Copy,
                                     accum_out=sums[:, 0, o:o + 1]).then_inc(converted, 1)
                nc.scalar.activation(squares, adj_in[:, o % 2, :], ACT.Square,
                                     accum_out=sums[:, 1, o:o + 1]).then_inc(adj_free, 1)

            def rank_rows(q):
                act.wait_ge(degs_spread, q + 1)
                for o in range(GT):
                    nc.scalar.activation(beaten[:, :], psR[:, :], ACT.Sign, bias=negkey[:, o:o + 1],
                                         accum_out=rank[:, o:o + 1]).then_inc(rank_step, 1)
                    act.wait_ge(rank_step, GT * q + o + 1)

            def copy_sorted(q, o):
                t = GT * q + o
                act.wait_ge(permuted, t + 3)
                act.sem_inc(act_passed, 1)
                nc.scalar.copy(srt[:, q * GT + o, :], psA[:, o % 2, 0:XCOL])
                nc.scalar.copy(own[:, q * GT + o, :], psA[:, o % 2, XCOL:REC])
                if o == 0:
                    for i in range(BANDS):
                        at = DIRECT + i * MORE
                        nc.scalar.copy(more[i * TOP:(i + 1) * TOP, :], psA[0:TOP, 0, at:at + MORE])
                nc.scalar.copy(idx[:, o, :], psA[:, o % 2, 0:LIST]).then_inc(sorted_copied, 1)

            def deviation(q, o):
                act.wait_ge(var_ready, GT * q + o + 1)
                nc.scalar.sqrt(std[:, :], mv[:, 1:2]).then_inc(std_ready, 1)

            def h_tile(q, o):
                t = GT * q + o
                act.wait_ge(x1_turned, t + 2)
                act.wait_ge(h_ready, t)
                nc.scalar.copy(x1T[:, :], psT[:, 0:P]).then_inc(x1T_copied, 1)
                act.wait_ge(h_ready, t + 1)
                act.wait_ge(row_stored[o], 16 * q)
                nc.scalar.activation(sgn[:, :], psH[:, D + 1:D + 2], ACT.Sign).then_inc(act_step, 1)
                nc.scalar.copy(hrow[:, o, 0:D + 1], psH[:, 0:D + 1]).then_inc(act_step, 1)
                nc.scalar.copy(hown[:, q * GT + o, 0:D], psH[:, 0:D]).then_inc(act_step, 1)
                nc.scalar.copy(hown[:, q * GT + o, D:D + 1], psH[:, D + 2:D + 3]).then_inc(act_step, 1)
                nc.scalar.copy(rid[:, o:o + 1], srt[:, q * GT + o, ROW:ROW + 1]).then_inc(act_step, 1)
                act.wait_ge(act_step, 5 * (t + 1))
                nc.scalar.square(v_own[:, bass.ds(t, 1)], sgn[:, :]).then_inc(hrow_ready, 1)
                act.wait_ge(hrow_ready, t + 1)
                act.sem_inc(h_saved, 1)

            def copy_spread(q):
                for i in range(2):
                    act.wait_ge(d_spread, 2 * q + i + 1)
                    at = q * GROWS + i * BANK
                    nc.scalar.copy(d_bc[:, at:at + BANK], psR[:, i * BANK:(i + 1) * BANK]).then_inc(d_bc_copied, 1)

            def max_group(q, last=False):
                if last:
                    for i in range(PAIRS):
                        nc.scalar.copy(adj_rid[:, i:i + 1], srt[:, i, ROW:ROW + 1]).then_inc(adj_rid_ready, 1)
                for o in range(GT):
                    converts = [] if last else list(range(CONVERTED[o - 1] if o else 0, CONVERTED[o]))
                    for i in converts[:1]:
                        convert(q + 1, i)
                    for i in PERMUTED[o]:
                        copy_sorted(q, i)
                    for i in converts[1:]:
                        convert(q + 1, i)
                    if o and not last:
                        h_tile(q, o - 1)
                    if last and o >= GT - 3:
                        copy_spread(o - (GT - 3))
                    if o == PLACE_AT and not last:
                        for i in range(2):
                            copy_sorted(q + 1, i)
                    deviation(q, o)
                    if last or o == GT - 1:
                        h_tile(q, o)
                    if o == SORT_AT and not last:
                        rank_rows(q + 1)

            def mask(q, i):
                b = i % 2
                act.wait_ge(rows_gathered[b], 16 * (PAIRS // 2 * q + i // 2 + 1))
                nc.scalar.activation(adj_in[:, b, :].bitcast(F32), adj_in[:, b, :], ACT.Copy, bias=FAR,
                                     scale=-FAR).then_inc(mask_ready, 1)

            def exponentials(q, i, part):
                n, b = PAIRS * q + i, i % 2
                masked = adj_in[:, b, :].bitcast(F32)
                if part == 0:
                    act.wait_ge(dense_logits_ready, n + 1)
                    act.wait_ge(w_turned, PIECES * n)
                    nc.scalar.activation(dense_w[b], masked, ACT.Exp, bias=shift[:, 0:1]).then_inc(dense_exp_ready, 1)
                else:
                    nc.scalar.activation(masked, masked, ACT.Exp, bias=shift[:, 1:2], scale=ALPHA
                                         ).then_inc(dense_exp_ready, 1)

            def spread_weights(q, i):
                n = PAIRS * q + i
                act.wait_ge(sparse_weights_ready, n + 1)
                act.wait_ge(buffer_free1, n + 2)
                for k in range(SLOTS[PAIRS + i]):
                    spread = nc.scalar.activation(weight_diag[:, k, :], ident[:, :], ACT.Copy, scale=wgt[:, k:k + 1])
                spread.then_inc(weight_diag_ready, 1)

            def finish(q, i):
                act.wait_ge(neg_ready, PAIRS * q + i + 3)
                nc.scalar.activation(uexp[:, :, :], uneg[:, :, :], ACT.Exp).then_inc(uexp_ready, 1)

            def deviations(q):
                for o in range(GT):
                    act.wait_ge(row_stored[o], 16 * (GROUPS + q))
                nc.scalar.copy(rid[:, :], srt[:, bass.ds(q * GT, GT), ROW]).then_inc(rid1_ready, 1)
                act.wait_ge(vars_ready, q + 1)
                nc.scalar.sqrt(stds[:, :], mvs[:, :, 1]).then_inc(stds_ready, 1)

            def sparse_exponentials(q, i):
                act.wait_ge(logits_ready, PAIRS * q + i + 1)
                K = SLOTS[PAIRS + i]
                nc.scalar.activation(p_exp[:, 0:K], em[:, 0:K], ACT.Exp, bias=nmx[:, :],
                                     accum_out=zs[:, 0:1]).then_inc(exp_ready, 1)

            def pair(q, i, before, last=False):
                n = PAIRS * q + i
                after = None if last and i + 1 == PAIRS else (q, i + 1) if i + 1 < PAIRS else (q + 1, 0)
                second = None if last and i + 2 >= PAIRS else (q, i + 2) if i + 2 < PAIRS else (q + 1, i + 2 - PAIRS)
                spread_weights(q, i)
                if after:
                    exponentials(*after, 0)
                if i and not last:
                    for j in [i - 1] if i + 1 < PAIRS else [i - 1, i]:
                        nc.scalar.copy(idx[:, PAIRS + j, :], srt[:, GT * q + (GT + PAIRS + j), 0:LIST]
                                       ).then_inc(idx1_ready, 1)
                        nc.scalar.copy(adj_rid[:, j:j + 1], srt[:, GT * q + (GT + j), ROW:ROW + 1]
                                       ).then_inc(adj_rid_ready, 1)
                for c in range(PIECES):
                    if c == 1 and before:
                        finish(*before)
                    if c == 1 and after:
                        exponentials(*after, 1)
                    if c == 2 and after:
                        sparse_exponentials(*after)
                    if c == 2 and second:
                        mask(*second)
                    act.wait_ge(w_turned, PIECES * (n + 1) + c + 1)
                    act.wait_ge(w_used, PIECES * n + c + 1)
                    nc.scalar.copy(wTs[c % 2], psP[c % 2][:, :]).then_inc(w_turn_copied, 1)
                if before and i == 0:
                    deviations(before[0])

            act.wait_ge(wT_ready, 1)
            nc.scalar.copy(wT[:, :], psW[:, 0:P]).then_inc(wT_copied, 1)
            act.wait_ge(wa_ready, 1)
            nc.scalar.copy(w_aug[:, D:D + 3], psW[:, P:P + 3]).then_inc(w_aug_ready, 1)

            for o in range(GT):
                convert(0, o)
            rank_rows(0)
            for o in range(2):
                copy_sorted(0, o)
            max_group(0)
            with act.Fori(1, GROUPS - 1) as q:
                max_group(q)
            max_group(GROUPS - 1, last=True)
            for i in range(PAIRS):
                nc.scalar.copy(idx[:, PAIRS + i, :], srt[:, PAIRS + i, 0:LIST]).then_inc(idx1_ready, 1)
            mask(0, 0)
            mask(0, 1)
            copy_spread(GROUPS - 1)
            act.wait_ge(keyed, TILES + 2)
            exponentials(0, 0, 0)
            exponentials(0, 0, 1)
            sparse_exponentials(0, 0)
            pair(0, 0, None)
            with act.Fori(0, GROUPS - 1) as q:
                for i in range(1, PAIRS):
                    pair(q, i, (q, i - 1))
                pair(q + 1, 0, (q, PAIRS - 1))
            for i in range(1, PAIRS):
                pair(GROUPS - 1, i, (GROUPS - 1, i - 1), last=True)
            finish(GROUPS - 1, PAIRS - 1)
            deviations(GROUPS - 1)

            def dense():
                with act.Fori(0, TILES) as t:
                    act.wait_ge(d_var_ready, t + 1)
                    nc.scalar.sqrt(std[:, :], mv[:, 1:2]).then_inc(d_std_ready, 1)
                    act.wait_ge(d_x1_turned, t + 1)
                    nc.scalar.copy(x1T[:, :], psT[:, 0:P]).then_inc(d_x1T_copied, 1)
                    act.wait_ge(d_h_ready, t + 1)
                    nc.scalar.copy(d_h[:, :], psH[:, 0:D + 3]).then_inc(act_step, 1)
                    nc.scalar.activation(sgn[:, :], psH[:, D + 1:D + 2], ACT.Sign).then_inc(act_step, 1)
                    act.wait_ge(act_step, 5 * TILES + 3 * t + 2)
                    nc.scalar.copy(s_all[:, bass.ds(t, 1)], d_h[:, D + 2:D + 3]).then_inc(act_step, 1)
                    nc.scalar.square(d_h[:, D + 1:D + 2], sgn[:, :]).then_inc(d_h_saved, 1)
                with act.Fori(0, TILES) as t:
                    act.wait_ge(e_logits_ready, t + 1)
                    nc.scalar.activation(d_p, d_z, ACT.Exp, bias=nmx[:, :], accum_out=zs[:, 0:1]
                                         ).then_inc(e_exp_ready, 1)
                    for c in range(TILES):
                        act.wait_ge(e_turned, TILES * t + c + 1)
                        nc.scalar.copy(d_wT[c % 2], psT[:, 0:P]).then_inc(e_turn_copied, 1)
                    act.wait_ge(e_neg_ready, t + 1)
                    nc.scalar.activation(uexp[:, 0, :], uneg[:, 0, :], ACT.Exp).then_inc(e_uexp_ready, 1)
                    act.wait_ge(e_var_ready, t + 1)
                    nc.scalar.sqrt(std[:, :], mv[:, 1:2]).then_inc(e_std_ready, 1)

            act.wait_ge(flag_ready, 1)
            with act.If(act.value_load(flag_int[0:1, 0:1], min_val=0, max_val=1) > 0):
                dense()

        @block.tensor
        def _(pe):
            pe.wait_ge(consts_dve, 4)
            pe.wait_ge(weights_loaded, 48)
            nc.tensor.transpose(psW[:, 0:P], w_aug[:, 0:D], ident[:, :]).then_inc(wT_ready, 1)
            pe.wait_ge(wT_copied, 1)
            nc.tensor.matmul(psW[:, P:P + 3], wT[:, :], a3[:, :], start=True, stop=True).then_inc(wa_ready, 1)
            pe.wait_ge(w_aug_ready, 1)

            def spread_degrees(q):
                pe.wait_ge(diag_ready, q + 1)
                for i in range(2):
                    mm = nc.tensor.matmul(psR[:, i * BANK:(i + 1) * BANK], ones[:, :],
                                          diag[:, 4 * i:4 * i + 4, :].rearrange("p o n -> p (o n)"),
                                          start=True, stop=True)
                mm.then_inc(degs_spread, 1)

            def max_tile(q, o):
                t = GT * q + o
                pe.wait_ge(x1_ready, t + 1)
                pe.wait_ge(x1T_copied, t + 1)
                nc.tensor.transpose(psT[:, 0:P], x1w[:, o, :], ident[:, :]).then_inc(x1_turned, 1)
                pe.wait_ge(x1T_copied, t + 2)
                pe.wait_ge(h_saved, t + 1)
                nc.tensor.matmul(psH[:, 0:D + 3], x1T[:, :], w_aug[:, :], start=True, stop=True).then_inc(h_ready, 1)

            def permute(q, o):
                t = GT * q + o
                if o == 0:
                    pe.wait_ge(sort_step, SORT_STEPS * (q + 1))
                    pe.wait_ge(x_loaded, 16 * (q + 1))
                pe.wait_ge(select_ready, t + 1)
                pe.wait_ge(sorted_copied, t + 1)
                for i in range(GT):
                    mm = nc.tensor.matmul(psA[:, o % 2, 0:REC], select[o % 2][:, i, :], rec[:, i, :],
                                          start=(i == 0), stop=(i == GT - 1))
                mm.then_inc(permuted, 1)

            pe.sem_inc(permuted, 2)
            pe.sem_inc(sorted_copied, 2)
            pe.sem_inc(x1T_copied, 1)
            pe.sem_inc(h_saved, 1)
            pe.sem_inc(x1_turned, 1)
            spread_degrees(0)
            for o in range(2):
                permute(0, o)
            with pe.Fori(0, GROUPS - 1) as q:
                for o in range(GT):
                    for i in PERMUTED[o]:
                        permute(q, i)
                    if o == SORT_AT + 1:
                        spread_degrees(q + 1)
                    if o:
                        max_tile(q, o - 1)
                    if o == PLACE_AT:
                        for i in range(2):
                            permute(q + 1, i)
                max_tile(q, GT - 1)
            def spread_h(q):
                pe.wait_ge(d_diag_ready, q + 1)
                if q:
                    pe.wait_ge(d_bc_copied, 2 * q)
                else:
                    pe.wait_ge(rank_step, TILES)
                for i in range(2):
                    nc.tensor.matmul(psR[:, i * BANK:(i + 1) * BANK], ones[:, :],
                                     diag[:, 4 * i:4 * i + 4, :].rearrange("p o n -> p (o n)"),
                                     start=True, stop=True).then_inc(d_spread, 1)

            for o in range(GT):
                for i in PERMUTED[o]:
                    permute(GROUPS - 1, i)
                if o >= GT - 3:
                    spread_h(o - (GT - 3))
                max_tile(GROUPS - 1, o)
            spread_h(GROUPS - 1)

            def turn(q, i, c):
                m = PIECES * (PAIRS * q + i) + c
                pe.wait_ge(w_turn_copied, m + 1)
                for k in range(PIECE // P):
                    at = c * PIECE + k * P
                    mm = nc.tensor.transpose(psP[c % 2][:, k * P:(k + 1) * P],
                                             dense_w[i % 2][:, at:at + P], ident[:, :])
                mm.then_inc(w_turned, 1)

            def weigh(q, i, c):
                m = PIECES * (PAIRS * q + i) + c
                pe.wait_ge(w_turn_copied, m + 3)
                for k in range(PIECE // P):
                    t = c * (PIECE // P) + k
                    mm = nc.tensor.matmul(psA[:, i % 2, 0:D], wTs[c % 2][:, k * P:(k + 1) * P], h_nat[:, t, 0:D],
                                          start=(t == 0), stop=(t == TILES - 1))
                mm.then_inc(w_used, 1)

            def weigh_sparse(q, i):
                n, K = PAIRS * q + i, SLOTS[PAIRS + i]
                pe.wait_ge(weight_diag_ready, n + 1)
                for k in range(K):
                    mm = nc.tensor.matmul(psS[i % 2][:, 0:D], weight_diag[:, k, :], gathered_h[i % 2][:, k, 0:D],
                                          start=(k == 0), stop=(k == K - 1))
                mm.then_inc(buffer_free1, 1)

            pe.wait_ge(d_bc_copied, 2 * GROUPS)
            pe.sem_inc(w_turn_copied, 2)
            pe.sem_inc(w_turned, PIECES)
            pe.sem_inc(w_used, 2)
            pe.sem_inc(neg_ready, 2)
            with pe.Fori(0, GROUPS) as q:
                for i in range(PAIRS):
                    n = PAIRS * q + i
                    weigh_sparse(q, i)
                    pe.wait_ge(dense_weights_ready, n + 1)
                    turn(q, i, 0)
                    pe.wait_ge(neg_ready, n + 1)
                    for c in range(PIECES):
                        if c + 1 < PIECES:
                            turn(q, i, c + 1)
                        weigh(q, i, c)
            pe.wait_ge(v_checked, 2)
            nc.tensor.matmul(psW[:, 0:GT], ones[:, :], flag_sum[:, :], start=True, stop=True).then_inc(flag_spread, 1)

            def dense():
                with pe.Fori(0, TILES) as t:
                    pe.wait_ge(d_x1_ready, t + 1)
                    nc.tensor.transpose(psT[:, 0:P], x1w[:, 0, :], ident[:, :]).then_inc(d_x1_turned, 1)
                    pe.wait_ge(d_x1T_copied, t + 1)
                    nc.tensor.matmul(psH[:, 0:D + 3], x1T[:, :], w_aug[:, :], start=True, stop=True
                                     ).then_inc(d_h_ready, 1)
                pe.wait_ge(d_rows_loaded, 48)
                pe.sem_inc(e_turn_copied, 1)
                with pe.Fori(0, TILES) as t:
                    pe.wait_ge(e_weights_ready, t + 1)
                    for c in range(TILES):
                        pe.wait_ge(e_turn_copied, TILES * t + c + 1)
                        nc.tensor.transpose(psT[:, 0:P], d_p[:, c * P:(c + 1) * P], ident[:, :]
                                            ).then_inc(e_turned, 1)
                        pe.wait_ge(e_turn_copied, TILES * t + c + 2)
                        mm = nc.tensor.matmul(psH[:, 0:D], d_wT[c % 2], h_rows[:, c, :],
                                              start=(c == 0), stop=(c == TILES - 1))
                    mm.then_inc(e_sum_ready, 1)

            pe.wait_ge(flag_ready, 1)
            with pe.If(pe.value_load(flag_int[0:1, 0:1], min_val=0, max_val=1) > 0):
                dense()

        @block.vector
        def _(dve):
            V = nc.vector
            dve.sem_inc(keyed, 2)
            dve.wait_ge(consts_pool, 7)
            V.tensor_scalar(ident[:, :], ident[:, :], 0.0, None, ALU.is_equal).then_inc(consts_dve, 1)
            V.memset(ones[:, :], 1.0).then_inc(consts_dve, 1)
            V.memset(a3[:, 1:2], 1.0).then_inc(consts_dve, 1)
            V.memset(flag_sum[:, :], 0.0).then_inc(consts_dve, 1)
            for o in range(GT):
                V.memset(slots_of[:, o:o + 1], float(SLOTS[o] if o else DIRECT)).then_inc(consts_dve, 1)
            dve.wait_ge(consts_dve, 4 + GT)
            V.memset(slots_of[0:TOP, 0:1], float(DIRECT + BANDS * MORE)).then_inc(consts_dve, 1)
            V.tensor_scalar(tile_base[:, :], tile_base[:, :], (GROWS - 1) / 2 + 1, None, ALU.add).then_inc(consts_dve, 1)
            dve.wait_ge(consts_dve, 6 + GT)

            def find(q, o, at, to):
                for s in range(at, to):
                    m = V.max(cand[:, o % 2, 8 * s:8 * s + 8], keys[:, s * SEGMENT:(s + 1) * SEGMENT])
                if to == SEGMENTS:
                    m.then_inc(found, 1)

            def extract(q, o):
                t = GT * q + o
                dve.wait_ge(converted, t + 1)
                dve.wait_ge(found, t)
                V.tensor_tensor(keys.rearrange("p (s c) -> p s c", s=SEGMENTS),
                                adj16[:, o % 2, :].rearrange("p (s c) -> p s c", s=SEGMENTS),
                                local_iota[:, :].unsqueeze(1).to_broadcast([P, SEGMENTS, SEGMENT]),
                                ALU.mult).then_inc(keyed, 1)
                dve.wait_ge(keyed, t + 3)
                dve.sem_inc(dve_passed, 1)
                if o == 0:
                    find(q, o, 0, SEGMENTS)
                else:
                    merge(q, o - 1, lambda k: find(q, o, min(k * 3 // 2, SEGMENTS),
                                                   SEGMENTS if k == EXTRACT_STEPS - 1 else min((k + 1) * 3 // 2, SEGMENTS)))
                if o == GT - 1:
                    merge(q, o)

            def merge(q, o, between=lambda k: None):
                step = Steps(dve, extract_step, EXTRACT_STEPS, GT * q + o)

                def then(instruction):
                    instruction.then_inc(extract_step, 1)
                    between(step.k)
                    step.k += 1
                    dve.wait_ge(extract_step, step.base + step.k)
                    dve.sem_inc(dve_passed, 1)

                c = cand[:, o % 2, :]
                if o == GT - 1:
                    dve.wait_ge(found, GT * q + o + 1)
                then(V.scalar_tensor_tensor(out=gkey[:, 1, :], in0=c, scalar=0.0, in1=seg_base[:, :],
                                            op0=ALU.is_gt, op1=ALU.mult))
                then(V.tensor_tensor(gkey[:, 0, :], gkey[:, 1, :], c, ALU.add))
                for r in range(LIST // 8):
                    eight = listed[:, o, 8 * r:8 * r + 8]
                    then(V.max(eight, gkey[:, r % 2, :]))
                    if r < LIST // 8 - 1:
                        then(V.match_replace(gkey[:, (r + 1) % 2, :], eight, gkey[:, r % 2, :], 0.0))
                step.end()

            def sort(q):
                step = Steps(dve, sort_step, SORT_STEPS, q)
                dve.wait_ge(permuted, GT * q + 2)
                dve.wait_ge(adj_free, GT * (q + 1) + 2)
                degs = rec[:, :, DEG]
                V.tensor_copy(rec[:, :, ROW], row_id[:, bass.ds(q * GT, GT)])
                step(V.tensor_scalar(filled[:, :, :], listed[:, :, :], 0.0, None, ALU.is_gt))
                step(V.tensor_reduce(degs, filled[:, :, :], AX.X, ALU.add))
                V.scalar_tensor_tensor(out=filled[:, :, :], in0=filled[:, :, :], scalar=0.0,
                                       in1=listed[:, :, 0:1].to_broadcast([P, GT, LIST]), op0=ALU.is_equal, op1=ALU.mult)
                V.tensor_tensor(flags[:, 0, :], sums[:, 0, :], degs, ALU.not_equal)
                V.tensor_tensor(flags[:, 1, :], sums[:, 1, :], degs, ALU.not_equal)
                step(V.scalar_tensor_tensor(out=degkey[:, :], in0=degs, scalar=float(GROWS), in1=tie[:, :],
                                            op0=ALU.mult, op1=ALU.add))
                V.tensor_tensor(diag[:, :, :], ident[:, :].unsqueeze(1).to_broadcast([P, GT, P]),
                                degkey[:, :].unsqueeze(2).to_broadcast([P, GT, P]), ALU.mult)
                step(V.tensor_scalar(negkey[:, :], degkey[:, :], -1.0, None, ALU.mult))
                dve.sem_inc(diag_ready, 1)
                step(V.tensor_tensor(filled[:, :, :], filled[:, :, :], listed[:, :, :], ALU.add))
                step(V.tensor_tensor(flag_sum[:, :], flag_sum[:, :], flags[:, 0, :], ALU.add))
                step(V.tensor_tensor(flag_sum[:, :], flag_sum[:, :], flags[:, 1, :], ALU.add))
                step(V.tensor_scalar(rec[:, :, 0:LIST], filled[:, :, :], -1.0, 0.0, ALU.add, ALU.max))
                step.end()

            def places(q):
                dve.wait_ge(rank_step, GT * (q + 1))
                V.scalar_tensor_tensor(out=place[:, :, :], in0=rank[:, :].unsqueeze(1).to_broadcast([P, GT, GT]),
                                       scalar=0.5, in1=tile_base[:, :].unsqueeze(2).to_broadcast([P, GT, GT]),
                                       op0=ALU.mult, op1=ALU.add).then_inc(place_step, 1)
                dve.wait_ge(place_step, q + 1)
                dve.sem_inc(dve_passed, 1)

            def selection(q, o):
                dve.wait_ge(permuted, GT * q + o + 1)
                V.tensor_tensor(select[o % 2][:, :, :], local_iota[:, 0:P].unsqueeze(1).to_broadcast([P, GT, P]),
                                place[:, o, :].unsqueeze(2).to_broadcast([P, GT, P]),
                                ALU.is_equal).then_inc(select_ready, 1)

            def check_slots(q):
                step = Steps(dve, check_step, CHECK_STEPS, q)
                dve.wait_ge(sorted_copied, GT * (q + 1) + 2)
                step(V.tensor_tensor(flags[:, 0, :], srt[:, bass.ds(q * GT, GT), DEG], slots_of[:, :], ALU.is_gt))
                step(V.tensor_tensor(flag_sum[:, :], flag_sum[:, :], flags[:, 0, :], ALU.add))
                step.end()

            def max_tile(q, o):
                t = GT * q + o
                K = SLOTS[o]
                step = Steps(dve, reduce_step, REDUCE_STEPS, t)
                dve.wait_ge(sorted_copied, t + 3)
                dve.sem_inc(dve_passed, 1)
                step(V.tensor_scalar(has[:, :], srt[:, q * GT + o, DEG:DEG + 1], 1.0, None, ALU.min))
                dve.wait_ge(gathered[o % 2], 16 * (q * PER_GROUP[o % 2] + UPTO[o]))
                if o == 0:
                    K = DIRECT
                    V.tensor_reduce(bands[:, 0, :], G[:, 0, K * D:(K + MORE) * D].rearrange("p (k d) -> p d k", d=D),
                                    AX.X, ALU.max)
                V.tensor_reduce(nmax[:, :], G[:, o % 2, 0:K * D].rearrange("p (k d) -> p d k", d=D),
                                AX.X, ALU.max).then_inc(buffer_free, 1)
                dve.wait_ge(buffer_free, t + 3)
                if o == 0:
                    link = Steps(dve, top_step, TOP_STEPS, q)
                    for i in range(1, BANDS):
                        copied = V.tensor_copy(bands[0:TOP, i, :], bands[i * TOP:(i + 1) * TOP, 0, :])
                    link(copied)
                    link(V.tensor_reduce(bands[0:TOP, BANDS, :], bands[0:TOP, 0:BANDS, :].rearrange("p k d -> p d k"),
                                         AX.X, ALU.max))
                    link(V.tensor_tensor(nmax[0:TOP, :], nmax[0:TOP, :], bands[0:TOP, BANDS, :], ALU.max))
                    link.end()
                step(V.scalar_tensor_tensor(out=y0[:, :], in0=nmax[:, :], scalar=has[:, :],
                                            in1=own[:, q * GT + o, :], op0=ALU.mult, op1=ALU.add))
                step(V.bn_stats(stats[:, 0, :], y0[:, :]), dve_passed)
                step(V.bn_aggr(mv[:, :], stats[:, 0, :]))
                V.tensor_scalar(mv[:, 1:2], mv[:, 1:2], EPS, None, ALU.add).then_inc(var_ready, 1)
                step.end()

            def norm_tile(q, o):
                t = GT * q + o
                step = Steps(dve, norm_tile_step, NORM_TILE_STEPS, t)
                dve.wait_ge(std_ready, t + 1)
                step(V.reciprocal(rstd[:, :], std[:, :]))
                dve.wait_ge(x1_turned, GT * q + 1)
                V.tensor_scalar(x1w[:, o, :], y0[:, :], mv[:, 0:1], rstd[:, :], ALU.subtract,
                                ALU.mult).then_inc(x1_ready, 1)
                dve.wait_ge(x1_ready, t + 1)
                dve.sem_inc(dve_passed, 1)
                step(V.tensor_copy(own[:, q * GT + o, :], x1w[:, o, :]))
                step.end()

            def dense_logits(q, i):
                n, b, s_own = PAIRS * q + i, i % 2, hown[:, GT * q + i, D:D + 1]
                link = Steps(dve, shift_step, SHIFT_STEPS, n)
                masked = adj_in[:, b, :].bitcast(F32)
                dve.wait_ge(dense_exp_ready, 2 * n)
                dve.wait_ge(mask_ready, n + 1)
                dve.sem_inc(dve_passed, 1)
                link(V.tensor_tensor_reduce(masked, masked, d_bc[:, :], 1.0, FMIN, ALU.add, ALU.max, mx[:, 1:2]))
                link(V.tensor_scalar(zmax[:, :], mx[:, 1:2], FAR / 50, s_own, ALU.max, ALU.add))
                link(V.scalar_tensor_tensor(out=emax[:, :], in0=zmax[:, :], scalar=ALPHA, in1=zmax[:, :],
                                            op0=ALU.mult, op1=ALU.max))
                V.tensor_tensor(shift[:, 0:1], s_own, emax[:, :], ALU.subtract)
                V.scalar_tensor_tensor(out=shift[:, 1:2], in0=s_own, scalar=ALPHA, in1=emax[:, :],
                                       op0=ALU.mult, op1=ALU.subtract).then_inc(dense_logits_ready, 1)
                link.end()

            def sparse_logits(q, i):
                n, b, K, sparse = PAIRS * q + i, i % 2, SLOTS[PAIRS + i], GT * q + (PAIRS + i)
                step = Steps(dve, sparse_logits_step, SPARSE_LOGITS_STEPS, n)
                dve.wait_ge(gathered1[b], 16 * (q * PER_GROUP1[b] + UPTO1[i]))
                V.tensor_scalar(pen[:, 0:K], slot_iota[:, 0:K], srt[:, sparse, DEG:DEG + 1], NEG, ALU.is_ge, ALU.mult)
                step(V.tensor_scalar(z[:, 0:K], gathered_h[b][:, 0:K, D], hown[:, sparse, D:D + 1], None, ALU.add))
                step(V.scalar_tensor_tensor(out=e[:, 0:K], in0=z[:, 0:K], scalar=ALPHA, in1=z[:, 0:K],
                                            op0=ALU.mult, op1=ALU.max), dve_passed)
                step(V.tensor_tensor_reduce(em[:, 0:K], e[:, 0:K], pen[:, 0:K], 1.0, FMIN, ALU.add, ALU.max,
                                            mx[:, 0:1]))
                V.tensor_scalar(nmx[:, :], mx[:, 0:1], -1.0, None, ALU.mult).then_inc(logits_ready, 1)
                step.end()

            def dense_weights(q, i, between):
                n, b = PAIRS * q + i, i % 2
                step = Steps(dve, weigh_step, WEIGH_STEPS, n)
                dve.wait_ge(dense_exp_ready, 2 * n + 2)
                dve.sem_inc(dve_passed, 1)
                step(V.scalar_tensor_tensor(out=dense_w[b], in0=dense_w[b], scalar=1.0,
                                            in1=adj_in[:, b, :].bitcast(F32), op0=ALU.mult, op1=ALU.max,
                                            accum_out=zs[:, 1:2]))
                dve.sem_inc(merged, 1)
                sparse_weights(q, i)
                step(V.tensor_scalar(zs[:, 1:2], zs[:, 1:2], 0.5, None, ALU.max))
                step(V.tensor_scalar(thz[:, :], zs[:, 1:2], THR, None, ALU.mult))
                between()
                V.scalar_tensor_tensor(out=dense_w[b], in0=dense_w[b], scalar=thz[:, :], in1=dense_w[b],
                                       op0=ALU.is_ge, op1=ALU.mult).then_inc(dense_weights_ready, 1)
                step.end()

            def dense_gate(q, i):
                dense = GT * q + i
                step = Steps(dve, gate_step, GATE_STEPS, PAIRS * q + i)
                step(V.reciprocal(rz[:, 1:2], zs[:, 1:2]))
                step(V.scalar_tensor_tensor(out=gate[:, 2:3], in0=rz[:, 1:2], scalar=THR, in1=srt[:, dense, DEG:DEG + 1],
                                            op0=ALU.is_gt, op1=ALU.mult))
                step(V.tensor_tensor(gate[:, 2:3], gate[:, 2:3], rz[:, 1:2], ALU.mult))
                step.end()

            def sparse_weights(q, i):
                n, b, K, sparse = PAIRS * q + i, i % 2, SLOTS[PAIRS + i], GT * q + (PAIRS + i)
                dve.wait_ge(exp_ready, n + 1)
                link = Steps(dve, sparse_step, SPARSE_STEPS, n)
                link(V.reciprocal(rz[:, 0:1], zs[:, 0:1]))
                V.scalar_tensor_tensor(out=gate[:, b:b + 1], in0=rz[:, 0:1], scalar=THR,
                                       in1=srt[:, sparse, DEG:DEG + 1], op0=ALU.is_gt, op1=ALU.mult)
                link(V.tensor_scalar(att[:, 0:K], p_exp[:, 0:K], rz[:, 0:1], None, ALU.mult))
                V.scalar_tensor_tensor(out=wgt[:, 0:K], in0=att[:, 0:K], scalar=THR, in1=att[:, 0:K],
                                       op0=ALU.is_ge, op1=ALU.mult).then_inc(sparse_weights_ready, 1)
                link.end()

            def finish(q, i, between=lambda: None):
                n = PAIRS * q + i
                step = Steps(dve, finish_step, FINISH_STEPS, n)
                dve.wait_ge(buffer_free1, n + 3)
                V.scalar_tensor_tensor(out=u[:, 1, :], in0=psS[i % 2][:, 0:D], scalar=gate[:, i % 2:i % 2 + 1],
                                       in1=hown[:, GT * q + (PAIRS + i), 0:D], op0=ALU.mult, op1=ALU.add)
                dve.wait_ge(w_used, PIECES * (n + 1) + 2)
                step(V.scalar_tensor_tensor(out=u[:, 0, :], in0=psA[:, i % 2, 0:D], scalar=gate[:, 2:3],
                                            in1=hown[:, GT * q + i, 0:D], op0=ALU.mult, op1=ALU.add))
                V.tensor_scalar(uneg[:, :, :], u[:, :, :], 0.0, None, ALU.min).then_inc(neg_ready, 1)
                step(V.tensor_scalar(upos[:, :, :], u[:, :, :], 0.0, None, ALU.max))
                between()
                dve.wait_ge(uexp_ready, n + 1)
                step(V.scalar_tensor_tensor(out=u[:, :, :], in0=uexp[:, :, :], scalar=-1.0, in1=upos[:, :, :],
                                            op0=ALU.add, op1=ALU.add))
                step(V.tensor_tensor(by_pair(yw)[:, i, :, :], u[:, :, :], by_pair(own)[:, i, bass.ds(2 * q, 2), :], ALU.add))
                V.bn_stats(stats[:, 0, :], yw[:, i, :])
                step(V.bn_stats(stats[:, 1, :], yw[:, PAIRS + i, :]), dve_passed)
                V.bn_aggr(mvs[:, i, :], stats[:, 0, :])
                step(V.bn_aggr(mvs[:, PAIRS + i, :], stats[:, 1, :]))
                step.end()

            def variances(q):
                V.tensor_scalar(mvs[:, :, 1], mvs[:, :, 1], EPS, None, ALU.add).then_inc(vars_ready, 1)

            def norm_group(q):
                step = Steps(dve, norm_step, NORM_STEPS, q)
                dve.wait_ge(stds_ready, q + 1)
                step(V.reciprocal(rstds[:, :], stds[:, :]))
                for o in range(GT):
                    dve.wait_ge(row_stored[o], 16 * (GROUPS + q))
                    V.tensor_scalar(normed[:, o, 0:D], yw[:, o, :], mvs[:, o, 0:1], rstds[:, o:o + 1], ALU.subtract,
                                    ALU.mult).then_inc(out_ready, 1)
                step.end()

            def pair(q, i, before, last=False, norm_before=True):
                after = None if last and i + 1 == PAIRS else (q, i + 1) if i + 1 < PAIRS else (q + 1, 0)

                def meanwhile():
                    dense_gate(q, i)
                    if after:
                        sparse_logits(*after)

                dense_weights(q, i, lambda: dense_logits(*after) if after else None)
                if i == 1 and norm_before:
                    norm_group(q - 1)
                if before:
                    finish(*before, meanwhile)
                else:
                    meanwhile()
                if before and i == 0:
                    variances(before[0])

            for o in range(GT):
                extract(0, o)
            sort(0)
            places(0)
            for o in range(2):
                selection(0, o)
            with dve.Fori(0, GROUPS - 1) as q:
                for o in range(GT):
                    for i in PERMUTED[o]:
                        selection(q, i)
                    for i in range(EXTRACTS[o]):
                        extract(q + 1, FIRST[o] + i)
                    if o:
                        norm_tile(q, o - 1)
                    if o == PLACE_AT:
                        places(q + 1)
                        for i in range(2):
                            selection(q + 1, i)
                    max_tile(q, o)
                    if o == SORT_AT:
                        sort(q + 1)
                norm_tile(q, GT - 1)
                check_slots(q)
            def diagonals(q):
                dve.wait_ge(h_nat_loaded[q], 16)
                if q:
                    dve.wait_ge(d_spread, 2 * q)
                else:
                    dve.wait_ge(permuted, TILES + 2)
                V.tensor_tensor(diag[:, :, :], ident[:, :].unsqueeze(1).to_broadcast([P, GT, P]),
                                h_nat[:, q * GT:(q + 1) * GT, D].unsqueeze(2).to_broadcast([P, GT, P]),
                                ALU.mult).then_inc(d_diag_ready, 1)

            for o in range(GT):
                for i in PERMUTED[o]:
                    selection(GROUPS - 1, i)
                if o >= GT - 3:
                    diagonals(o - (GT - 3))
                max_tile(GROUPS - 1, o)
                norm_tile(GROUPS - 1, o)
            check_slots(GROUPS - 1)
            dve.wait_ge(hrow_ready, TILES)
            V.tensor_reduce(least[:, :], v_own[:, :], AX.X, ALU.min).then_inc(v_checked, 1)
            dve.wait_ge(v_checked, 1)
            V.scalar_tensor_tensor(out=flag_sum[:, 0:1], in0=least[:, :], scalar=0.0, in1=flag_sum[:, 0:1],
                                   op0=ALU.is_equal, op1=ALU.add).then_inc(v_checked, 1)
            diagonals(GROUPS - 1)
            dve.wait_ge(d_bc_copied, 2 * GROUPS)
            dense_logits(0, 0)
            sparse_logits(0, 0)
            pair(0, 0, None)
            pair(0, 1, (0, 0), norm_before=False)
            with dve.Fori(0, GROUPS - 1) as q:
                for i in range(2, PAIRS):
                    pair(q, i, (q, i - 1))
                pair(q + 1, 0, (q, PAIRS - 1))
                pair(q + 1, 1, (q + 1, 0))
            for i in range(2, PAIRS):
                pair(GROUPS - 1, i, (GROUPS - 1, i - 1), last=True)
            finish(GROUPS - 1, PAIRS - 1)
            variances(GROUPS - 1)
            norm_group(GROUPS - 1)
            dve.wait_ge(flag_spread, 1)
            V.reduce_max(flag[:, :], psW[:, 0:GT], axis=AX.X).then_inc(flag_checked, 1)
            dve.wait_ge(flag_checked, 1)
            V.tensor_scalar(flag_int[:, :], flag[:, :], 1.0, None, ALU.min).then_inc(flag_ready, 1)

            def dense_max(t):
                step = Steps(dve, d_max_step, DENSE_MAX_STEPS, t)
                dve.wait_ge(d_tile_loaded, 32 * (t + 1))
                V.tensor_scalar(d_bias, d_adj, 0.0, FMIN, ALU.is_equal, ALU.mult)
                V.memset(d_acc[:, :], FMIN)
                step(V.tensor_scalar(d_sum, d_adj, 0.0, 0.0, ALU.not_equal, ALU.add, accum_out=cnt[:, :]))
                step(V.tensor_scalar(d_has[:, :], cnt[:, :], 1.0, None, ALU.min), dve_passed)
                with dve.Fori(0, CHUNKS // 2) as c:
                    for b in range(2):
                        chunk = t * CHUNKS + c * 2 + b
                        link = Steps(dve, d_chunk_step, CHUNK_STEPS, chunk)
                        dve.wait_ge(d_chunk_loaded[b], 16 * (t * (CHUNKS // 2) + c + 1))
                        summed = d_sum.rearrange("p (j d) -> p j d", d=D)
                        V.tensor_tensor(summed, G[:, b, 0:CHUNK * D].rearrange("p (j d) -> p j d", d=D),
                                        d_bias[:, bass.ds((c * 2 + b) * CHUNK, CHUNK)].unsqueeze(2)
                                        .to_broadcast([P, CHUNK, D]), ALU.add).then_inc(d_chunk_used, 1)
                        dve.wait_ge(d_chunk_used, chunk + 3)
                        link(V.tensor_reduce(d_max[:, :], d_sum.rearrange("p (j d) -> p d j", d=D), AX.X, ALU.max))
                        link(V.tensor_tensor(d_acc[:, :], d_acc[:, :], d_max[:, :], ALU.max))
                        link.end()
                step(V.scalar_tensor_tensor(out=y0[:, :], in0=d_acc[:, :], scalar=d_has[:, :], in1=d_x[:, :],
                                            op0=ALU.mult, op1=ALU.add))
                step(V.bn_stats(stats[:, 0, :], y0[:, :]), dve_passed)
                step(V.bn_aggr(mv[:, :], stats[:, 0, :]))
                V.tensor_scalar(mv[:, 1:2], mv[:, 1:2], EPS, None, ALU.add).then_inc(d_var_ready, 1)
                dve.wait_ge(d_std_ready, t + 1)
                step(V.reciprocal(rstd[:, :], std[:, :]))
                V.tensor_scalar(x1w[:, 0, :], y0[:, :], mv[:, 0:1], rstd[:, :], ALU.subtract,
                                ALU.mult).then_inc(d_x1_ready, 1)
                step.end()

            def dense_attend(t):
                step = Steps(dve, e_step, DENSE_ATTEND_STEPS, t)
                dve.wait_ge(e_tile_loaded, 48 * (t + 1))
                step(V.scalar_tensor_tensor(out=d_vm, in0=d_adj, scalar=0.0, in1=v_rows, op0=ALU.is_gt, op1=ALU.mult))
                step(V.reduce_sum(cnt[:, :], d_vm, axis=AX.X))
                step(V.tensor_scalar(d_p, d_rows, s_all[:, bass.ds(t, 1)], None, ALU.add))
                step(V.scalar_tensor_tensor(out=d_z, in0=d_p, scalar=ALPHA, in1=d_p, op0=ALU.mult, op1=ALU.max))
                step(V.tensor_tensor(d_z, d_z, d_vm, ALU.mult))
                step(V.tensor_scalar(d_p, d_vm, 1.0, -NEG, ALU.subtract, ALU.mult))
                step(V.tensor_tensor(d_z, d_z, d_p, ALU.add))
                step(V.reduce_max(mx[:, 0:1], d_z, axis=AX.X))
                V.tensor_scalar(nmx[:, :], mx[:, 0:1], -1.0, None, ALU.mult).then_inc(e_logits_ready, 1)
                dve.wait_ge(e_exp_ready, t + 1)
                step(V.reciprocal(rz[:, 0:1], zs[:, 0:1]))
                step(V.scalar_tensor_tensor(out=d_z, in0=d_p, scalar=rz[:, 0:1], in1=d_vm, op0=ALU.mult, op1=ALU.mult))
                step(V.reduce_max(topa[:, :], d_z, axis=AX.X))
                step(V.scalar_tensor_tensor(out=gate[:, 0:1], in0=topa[:, :], scalar=THR, in1=cnt[:, :],
                                            op0=ALU.is_gt, op1=ALU.mult))
                V.scalar_tensor_tensor(out=d_p, in0=d_z, scalar=THR, in1=d_z, op0=ALU.is_ge,
                                       op1=ALU.mult).then_inc(e_weights_ready, 1)
                dve.wait_ge(e_sum_ready, t + 1)
                step(V.tensor_scalar(hsum[:, :], psH[:, 0:D], gate[:, 0:1], None, ALU.mult))
                step(V.tensor_tensor(u[:, 0, :], hsum[:, :], h_own[:, :], ALU.add))
                V.tensor_scalar(uneg[:, 0, :], u[:, 0, :], 0.0, None, ALU.min).then_inc(e_neg_ready, 1)
                step(V.tensor_scalar(upos[:, 0, :], u[:, 0, :], 0.0, None, ALU.max))
                dve.wait_ge(e_uexp_ready, t + 1)
                step(V.scalar_tensor_tensor(out=u[:, 0, :], in0=uexp[:, 0, :], scalar=-1.0, in1=upos[:, 0, :],
                                            op0=ALU.add, op1=ALU.add))
                step(V.tensor_tensor(y0[:, :], u[:, 0, :], d_x[:, :], ALU.add))
                step(V.bn_stats(stats[:, 0, :], y0[:, :]), dve_passed)
                step(V.bn_aggr(mv[:, :], stats[:, 0, :]))
                V.tensor_scalar(mv[:, 1:2], mv[:, 1:2], EPS, None, ALU.add).then_inc(e_var_ready, 1)
                dve.wait_ge(e_std_ready, t + 1)
                step(V.reciprocal(rstd[:, :], std[:, :]))
                V.tensor_scalar(yw[:, 0, :], y0[:, :], mv[:, 0:1], rstd[:, :], ALU.subtract,
                                ALU.mult).then_inc(e_y_ready, 1)
                step.end()

            def dense():
                dve.sem_inc(d_chunk_used, 2)
                for o in range(GT):
                    dve.wait_ge(row_stored[o], 16 * 2 * GROUPS)
                with dve.Fori(0, TILES) as t:
                    dense_max(t)
                dve.wait_ge(d_rows_loaded, 48)
                with dve.Fori(0, TILES) as t:
                    dense_attend(t)

            dve.wait_ge(flag_ready, 1)
            with dve.If(dve.value_load(flag_int[0:1, 0:1], min_val=0, max_val=1) > 0):
                dense()


_INS = ['x', 'adj', 'L1_gnn_W', 'L1_gnn_a']


def kernel(**inputs):
    import numpy as _np
    import concourse.bacc as _bacc
    from concourse import mybir as _mybir
    from concourse.bass_utils import run_bass_kernel_spmd as _run

    nc = _bacc.Bacc("TRN2", target_bir_lowering=False, num_devices=1)
    arrays, args = {}, []
    for name in _INS:
        a = _np.ascontiguousarray(inputs[name])
        arrays[f"in_{name}_dram"] = a
        args.append(nc.dram_tensor(f"in_{name}_dram", a.shape, _mybir.dt.from_np(a.dtype), kind="ExternalInput").ap())
    args.append(nc.dram_tensor("out_0_dram", (N, D), _mybir.dt.float32, kind="ExternalOutput").ap())
    args.append(nc.dram_tensor("htab_dram", (N, HCOLS), _mybir.dt.float32, kind="Internal").ap())
    for name, cols in ("x1_dram", D), ("h_dram", D), ("d_dram", 1), ("v_dram", 1):
        args.append(nc.dram_tensor(name, (N, cols), _mybir.dt.float32, kind="Internal").ap())
    build(nc, *args)
    r = _run(nc, [arrays], core_ids=[0])
    return r.results[0]["out_0_dram"]
```
